# Optimizing a Trainium2 kernel written in Bass

```python
import numpy as np
import jax
import jax.numpy as jnp

def _softmax(x, axis=-1):
    return jax.nn.softmax(x, axis=axis)

def _gelu(x):
    return jax.nn.gelu(x, approximate=True)

def _silu(x):
    return jax.nn.silu(x)

def _sigmoid(x):
    return jax.nn.sigmoid(x)

def _layernorm(x, axis=-1, eps=1e-05):
    m = jnp.mean(x, axis=axis, keepdims=True)
    v = jnp.var(x, axis=axis, keepdims=True)
    return (x - m) / jnp.sqrt(v + eps)

def _scatter_add(tgt, idx, src, axis=0):
    return tgt.at[idx].add(src)

def _segment_sum(src, seg, n):
    return jax.ops.segment_sum(src, seg, n)
kernel_name = 'mk_sandwich_d1_jaxref_r8_17b569'

def setup_inputs(seed: int=0):
    np.random.seed(seed)
    _w = jnp.asarray

    def _L0_attn_setup():
        import jax, jax.numpy as jnp
        import numpy as np
        K_FACTOR = 0.5
        key = jax.random.key(seed)
        k1, k2, k3, k4 = jax.random.split(key, 4)
        B, S, H, I = (1, 256, 512, 1376)
        x = jax.random.normal(k1, (B, S, H), dtype=jnp.float32)
        w_gate = jax.random.normal(k2, (I, H), dtype=jnp.float32) * 0.02
        w_up = jax.random.normal(k3, (I, H), dtype=jnp.float32) * 0.02
        w_down = jax.random.normal(k4, (H, I), dtype=jnp.float32) * 0.02
        return {'x': x, 'w_gate': w_gate, 'w_up': w_up, 'w_down': w_down}
    _L0_attn_in = _L0_attn_setup()

    def _L0_ffn_setup():
        import jax, jax.numpy as jnp
        import numpy as np
        BLOCK = 128

        def weight_dequant(w, scale, block=BLOCK):
            O, I = w.shape
            wb = w.reshape(O // block, block, I // block, block)
            return (wb * scale[:, None, :, None]).reshape(O, I)
        key = jax.random.key(seed)
        k1, k2, k3 = jax.random.split(key, 3)
        B, S, D_IN, D_OUT = (4, 256, 512, 512)
        x = jax.random.normal(k1, (B, S, D_IN), dtype=jnp.float32)
        weight = jax.random.normal(k2, (D_OUT, D_IN), dtype=jnp.float32)
        weight_scale = jax.random.uniform(k3, (D_OUT // BLOCK, D_IN // BLOCK), dtype=jnp.float32, minval=0.5, maxval=1.5)
        return {'x': x, 'weight': weight, 'weight_scale': weight_scale}
    _L0_ffn_in = _L0_ffn_setup()
    _d = {'L0_attn_x': _L0_attn_in['x'], 'L0_attn_w_gate': _L0_attn_in['w_gate'], 'L0_attn_w_up': _L0_attn_in['w_up'], 'L0_attn_w_down': _L0_attn_in['w_down'], 'L0_ffn_weight': _L0_ffn_in['weight'], 'L0_ffn_weight_scale': _L0_ffn_in['weight_scale']}
    _x0 = _d['L0_attn_x']
    _d['L0_attn_x'] = jax.random.normal(jax.random.fold_in(jax.random.key(seed), 1), (1, 2048, 512), dtype=_x0.dtype)
    del _x0
    return _d

def reference(L0_attn_x, L0_attn_w_gate, L0_attn_w_up, L0_attn_w_down, L0_ffn_weight, L0_ffn_weight_scale):

    def _L0_attn_ref(x, w_gate, w_up, w_down):
        import jax, jax.numpy as jnp
        import numpy as np
        K_FACTOR = 0.5
        s = jax.nn.silu(jnp.einsum('bsh,ih->bsi', x, w_gate))
        B, S, I = s.shape
        k = int(K_FACTOR * I)
        _, idx = jax.lax.top_k(-jnp.abs(s), k)
        flat = s.reshape(B * S, I)
        rows = jnp.arange(B * S)[:, None]
        flat = flat.at[rows, idx.reshape(B * S, k)].set(0.0)
        s = flat.reshape(B, S, I)
        s = s * jnp.einsum('bsh,ih->bsi', x, w_up)
        return jnp.einsum('bsi,hi->bsh', s, w_down)

    def _L0_ffn_ref(x, weight, weight_scale):
        import jax, jax.numpy as jnp
        import numpy as np
        BLOCK = 128

        def weight_dequant(w, scale, block=BLOCK):
            O, I = w.shape
            wb = w.reshape(O // block, block, I // block, block)
            return (wb * scale[:, None, :, None]).reshape(O, I)
        w = weight_dequant(weight, weight_scale)
        return jnp.einsum('bsi,oi->bso', x, w)
    x = L0_attn_x
    x = x + _layernorm(_L0_attn_ref(_layernorm(x, axis=-1), L0_attn_w_gate, L0_attn_w_up, L0_attn_w_down), axis=-1)
    x = x + _layernorm(_L0_ffn_ref(_layernorm(x, axis=-1), L0_ffn_weight, L0_ffn_weight_scale), axis=-1)
    return x

_drawn_inputs = setup_inputs


def setup_inputs(seed=0):
    import zlib

    import numpy as np

    out = dict(_drawn_inputs(seed))
    spreads = {}
    factors = {}
    for name, (base, spread) in spreads.items():
        noise = np.random.default_rng([zlib.crc32(name.encode()), seed]).standard_normal(out[name].shape)
        drawn = base * np.exp(spread * noise) if base else spread * noise
        out[name] = jnp.asarray(drawn.astype(out[name].dtype))
    for name, factor in factors.items():
        out[name] = (out[name] * factor).astype(out[name].dtype)
    return out
```

```python
from contextlib import ExitStack

import concourse.bass as bass
from concourse import mybir

ALU = mybir.AluOpType
ACT = mybir.ActivationFunctionType
F32 = mybir.dt.float32
F32R = mybir.dt.float32r
BF16 = mybir.dt.bfloat16
I32 = mybir.dt.int32
I8 = mybir.dt.int8

P = 128
BANK = 512
EPS = 1e-5

MEDIAN_PER_MEAN = 0.8145
SPACING_PER_MEAN = 1.2666e-3
GAINS = (1.0, 0.8, 0.5, 0.4, 0.35)
COUNTS = len(GAINS) + 1
WINDOW = 8


def sandwich_kernel(nc: bass.Bass, x: bass.AP, w_gate_t: bass.AP, w_up_t: bass.AP, w_down_t: bass.AP,
                    w_lin_t: bass.AP, lin_scale_t: bass.AP, out: bass.AP):
    TOKENS, H = x.shape
    INNER = w_gate_t.shape[1]
    TILES = TOKENS // P
    KC = H // P
    DROP = INNER // 2
    BLOCKS = -(-INNER // P)
    LAST = INNER - (BLOCKS - 1) * P
    BANKS = [(b, min(BANK, INNER - b)) for b in range(0, INNER, BANK)]
    GROUPS = [(b, min(4, BLOCKS - b)) for b in range(0, BLOCKS, 4)]
    NG = len(GROUPS)
    PADS = WINDOW - 1
    assert H == BANK and LAST % 32 == 0 and INNER % 2 == 0 and TILES % 2 == 0 and TILES >= 6

    x_tiles = x.rearrange("(n p) h -> n p h", p=P)
    out_tiles = out.rearrange("(n p) h -> n p h", p=P)

    with ExitStack() as ctx:
        def sb(name, shape, dt):
            return ctx.enter_context(nc.sbuf_tensor(name, shape, dt))

        def ps(name, width):
            return ctx.enter_context(nc.psum_tensor(name, [P, width], F32))

        def sem(name):
            return ctx.enter_context(nc.semaphore(name))

        low_at = -(-nc.sbuf_base // 32) * 32
        low_size = (2 * KC * INNER + BLOCKS * H + KC * H)
        weights_low = sb("weights_low", [P, low_size], F32)
        taken = [0]

        def raw_and_low(name, shape):
            words = shape[1] * shape[2]
            raw = weights_low[:, taken[0]:taken[0] + words].rearrange("p (c n) -> p c n", c=shape[1])
            low = nc.alloc_sbuf_tensor_at(name + "_lo", shape, F32R, offset=low_at + 4 * taken[0])
            taken[0] += words
            return raw, low

        gate_raw, gate_lo = raw_and_low("gate", [P, KC, INNER])
        up_raw, up_lo = raw_and_low("up", [P, KC, INNER])
        down_raw, down_lo = raw_and_low("down", [P, BLOCKS, H])
        lin_raw, lin_lo = raw_and_low("lin", [P, KC, H])
        gate_hi = sb("gate_hi", [P, KC, INNER], F32R)
        up_hi = sb("up_hi", [P, KC, INNER], F32R)
        down_hi = sb("down_hi", [P, BLOCKS, H], F32R)
        lin_hi = sb("lin_hi", [P, KC, H], F32R)
        lin_scale = sb("lin_scale", [P, KC * KC], F32)

        x_in = sb("x_in", [P, 2, H], F32)
        x_res = sb("x_res", [P, 2, H], F32)
        xT_hi = sb("xT_hi", [P, H], F32R)
        xT_lo = sb("xT_lo", [P, H], F32R)
        gated = sb("gated", [P, 2, INNER], F32)
        mag = sb("mag", [P, 2, INNER + WINDOW], F32)
        signs = sb("signs", [P, INNER + PADS], I8)
        masked = sb("masked", [P, INNER], F32)
        mT_hi = sb("mT_hi", [P, BLOCKS * P], F32R)
        mT_lo = sb("mT_lo", [P, BLOCKS * P], F32R)
        normed = sb("normed", [P, H], F32)
        x2_hat = sb("x2_hat", [P, H], F32)
        x2T_hi = sb("x2T_hi", [P, H], F32R)
        x2T_lo = sb("x2T_lo", [P, H], F32R)
        ident = sb("ident", [P, P], F32)
        ones = sb("ones", [P, 1], F32)
        eps_col = sb("eps_col", [P, 1], F32)
        neg_half = sb("neg_half", [P, 1], F32)

        thr = sb("thr", [P, 1], F32)
        thr_new = sb("thr_new", [P, 1], F32)
        moves = sb("moves", [P, 1], I32)
        mag_sum = sb("mag_sum", [P, 1], F32)
        step_unit = sb("step_unit", [P, len(GAINS)], F32)
        step = sb("step", [P, len(GAINS)], F32)
        signed = sb("signed", [P, 1], F32)
        slot_of = sb("slot_of", [P, WINDOW], F32)
        top = sb("top", [P, 1 + WINDOW], F32)
        pick = sb("pick", [P, 2, WINDOW], F32)
        drop_at = sb("drop_at", [P, 1], F32)
        above = sb("above", [P, 1], F32)
        tied = sb("tied", [P, 1], F32)
        bad = sb("bad", [P, 1], F32)
        bad_rows = sb("bad_rows", [1, 1], I32)
        exact = sb("exact", [P, 1], I32)
        trial = sb("trial", [P, 1], I32)
        bit = sb("bit", [P, 1], I32)
        at_least = sb("at_least", [P, 1], F32)
        carry = sb("carry", [P, 1], F32)

        class Stats:

            def __init__(self, name):
                self.parts = sb(name + "_parts", [P, 6], F32)
                self.mean_var = sb(name + "_mean_var", [P, 2], F32)
                self.var_eps = sb(name + "_var_eps", [P, 1], F32)
                self.rstd = sb(name + "_rstd", [P, 1], F32)
                self.taken = sem(name + "_stats_taken")
                self.ready = sem(name + "_rstd_ready")

        ln_in, ln_mlp, ln_mid, ln_lin = (Stats("ln_" + n) for n in ("in", "mlp", "mid", "lin"))

        ps_gate = ps("ps_gate", 3 * BANK)
        ps_up = ps("ps_up", 3 * BANK)
        ps_x = ps("ps_x", BANK)
        ps_down = ps("ps_down", BANK)
        FLAG = 3 * BANK - 1
        flag_sum = ps_gate[0:1, FLAG:FLAG + 1]

        gate_loaded = [sem(f"gate_loaded{c}") for c in range(KC)]
        up_loaded = [sem(f"up_loaded{c}") for c in range(KC)]
        down_loaded = sem("down_loaded")
        lin_loaded = sem("lin_loaded")
        x_in_loaded = [sem(f"x_in_loaded{b}") for b in range(2)]
        x_res_loaded = [sem(f"x_res_loaded{b}") for b in range(2)]
        out_stored = [sem(f"out_stored{b}") for b in range(2)]
        gate_hi_ready, gate_lo_ready = sem("gate_hi_ready"), sem("gate_lo_ready")
        up_hi_ready, up_lo_ready = sem("up_hi_ready"), sem("up_lo_ready")
        down_hi_ready, down_lo_ready = sem("down_hi_ready"), sem("down_lo_ready")
        lin_scaled, lin_hi_ready, lin_lo_ready = sem("lin_scaled"), sem("lin_hi_ready"), sem("lin_lo_ready")
        pool_set, ident_ready, consts_ready = sem("pool_set"), sem("ident_ready"), sem("consts_ready")
        x_hat_ready = sem("x_hat_ready")
        xT_done, xT_hi_ready, xT_lo_ready = sem("xT_done"), sem("xT_hi_ready"), sem("xT_lo_ready")
        gate_done, up_done = sem("gate_done"), sem("up_done")
        silu_ready, mag_ready = sem("silu_ready"), sem("mag_ready")
        thr_ready, counted = sem("thr_ready"), sem("counted")
        bad_ready, flag_done = sem("bad_ready"), sem("flag_done")
        product_ready, masked_ready = sem("product_ready"), sem("masked_ready")
        mT_done, mT_hi_ready, mT_lo_ready = sem("mT_done"), sem("mT_hi_ready"), sem("mT_lo_ready")
        down_done, down_read = sem("down_done"), sem("down_read")
        x2_hat_ready = sem("x2_hat_ready")
        x2T_done, x2T_hi_ready, x2T_lo_ready = sem("x2T_done"), sem("x2T_hi_ready"), sem("x2T_lo_ready")
        lin_done, lin_read, out_ready = sem("lin_done"), sem("lin_read"), sem("out_ready")

        def each_iteration(eng, iteration):
            def known(i):
                iteration(i, i % 2, lambda d: 0 <= i + d < TILES)
            known(0)
            known(1)
            with eng.Fori(1, TILES // 2 - 1) as pair:
                for b in range(2):
                    iteration(pair * 2 + b, b, lambda d: True)
            for i in range(TILES - 2, TILES + 2):
                known(i)

        def wait(eng, semaphore, value):
            if not isinstance(value, int) or value > 0:
                eng.wait_ge(semaphore, value)

        block = ctx.enter_context(nc.Block())

        @block.sync
        def _(sp):
            def load_x_in(n, b):
                sp.dma_start(x_in[:, b, :], x_tiles[n]).then_inc(x_in_loaded[b], 16)

            def load_x_res(n, b):
                sp.dma_start(x_res[:, b, :], x_tiles[n]).then_inc(x_res_loaded[b], 16)

            load_x_in(0, 0)
            for c in range(KC):
                sp.dma_start(gate_raw[:, c, :], w_gate_t[c * P:(c + 1) * P, :]).then_inc(gate_loaded[c], 16)
            load_x_in(1, 1)
            for c in range(KC):
                sp.dma_start(up_raw[:, c, :], w_up_t[c * P:(c + 1) * P, :]).then_inc(up_loaded[c], 16)
            full = (BLOCKS - 1) * P
            sp.dma_start(down_raw[:, 0:BLOCKS - 1, :],
                         w_down_t[0:full, :].rearrange("(c p) h -> p c h", p=P)).then_inc(down_loaded, 16)
            sp.dma_start(down_raw[0:LAST, BLOCKS - 1, :], w_down_t[full:INNER, :]).then_inc(down_loaded, 16)
            load_x_res(0, 0)
            load_x_res(1, 1)
            sp.dma_start(lin_scale[:, :], lin_scale_t.rearrange("(o n) -> o n", o=1).to_broadcast([P, KC * KC])
                         ).then_inc(lin_loaded, 16)
            sp.dma_start(lin_raw[:, :, :], w_lin_t.rearrange("(c p) h -> p c h", p=P)).then_inc(lin_loaded, 16)

            def iteration(i, b, has):
                if has(2):
                    sp.wait_ge(xT_done, i + 1)
                    load_x_in(i + 2, b)
                if has(-2):
                    sp.wait_ge(out_ready, i - 1)
                    sp.dma_start(out_tiles[i - 2], x_res[:, b, :]).then_inc(out_stored[b], 16)
                    if has(0):
                        sp.wait_ge(out_stored[b], (i - b) * 8)
                        load_x_res(i, b)

            each_iteration(sp, iteration)
            for b in range(2):
                sp.wait_ge(out_stored[b], 16 * (TILES // 2))

        @block.gpsimd
        def _(pool):
            nc.gpsimd.memset(ident[:, :], 0.0).then_inc(pool_set, 1)
            nc.gpsimd.memset(eps_col[:, :], EPS).then_inc(pool_set, 1)
            nc.gpsimd.memset(neg_half[:, :], -0.5).then_inc(pool_set, 1)
            pool.wait_ge(pool_set, 3)
            nc.gpsimd.affine_select(out=ident[:, :], in_=ident[:, :], compare_op=ALU.not_equal, fill=1.0, base=0,
                                    pattern=[[-1, P]], channel_multiplier=1).then_inc(ident_ready, 1)

            def rstd(ln, n):
                pool.wait_ge(ln.taken, n + 1)
                nc.gpsimd.tensor_tensor(ln.var_eps[:, :], ln.mean_var[:, 1:2], eps_col[:, :], ALU.add)
                pool.drain()
                nc.gpsimd.tensor_tensor(ln.rstd[:, :], ln.var_eps[:, :], neg_half[:, :], ALU.pow).then_inc(ln.ready, 1)

            def low_part(lo, raw, hi):
                return nc.gpsimd.tensor_tensor(lo, raw, hi.bitcast(F32), ALU.subtract)

            def iteration(i, b, has):
                if has(-2):
                    rstd(ln_mlp, i - 2)
                    rstd(ln_mid, i - 2)
                if has(1):
                    rstd(ln_in, i + 1)
                if has(-2):
                    rstd(ln_lin, i - 2)
                    pool.wait_ge(lin_read, i - 1)
                    nc.gpsimd.tensor_tensor(x_res[:, b, :], x_res[:, b, :], normed[:, :],
                                            ALU.add).then_inc(out_ready, 1)

            rstd(ln_in, 0)

            def low_parts():
                for n, (c0, c1) in enumerate(((0, 5), (5, BLOCKS - 1))):
                    pool.wait_ge(down_hi_ready, n + 1)
                    low_part(down_lo[:, c0:c1, :], down_raw[:, c0:c1, :], down_hi[:, c0:c1, :])
                pool.wait_ge(down_hi_ready, 3)
                low_part(down_lo[0:LAST, BLOCKS - 1, :], down_raw[0:LAST, BLOCKS - 1, :],
                         down_hi[0:LAST, BLOCKS - 1, :]).then_inc(down_lo_ready, 1)
                pool.wait_ge(lin_loaded, 32)
                lin_blocks = lin_raw.rearrange("p c (o n) -> p (c o) n", n=P)
                nc.gpsimd.tensor_tensor(lin_blocks, lin_blocks,
                                        lin_scale[:, :].unsqueeze(2).to_broadcast([P, KC * KC, P]),
                                        ALU.mult).then_inc(lin_scaled, 1)
                pool.wait_ge(lin_hi_ready, 1)
                low_part(lin_lo[:, :, :], lin_raw, lin_hi[:, :, :]).then_inc(lin_lo_ready, 1)

            def with_low_parts(i, b, has):
                iteration(i, b, has)
                if isinstance(i, int) and i == 0:
                    low_parts()

            each_iteration(pool, with_low_parts)

        @block.scalar
        def _(act):
            def high_part(hi, src):
                return nc.scalar.activation(hi, src, ACT.Copy)

            def gate_high(c):
                act.wait_ge(gate_loaded[c], 16)
                high_part(gate_hi[:, c, :], gate_raw[:, c, :]).then_inc(gate_hi_ready, 1)

            def xT_high(n):
                act.wait_ge(xT_done, n + 1)
                high_part(xT_hi[:, :], ps_x[:, :]).then_inc(xT_hi_ready, 1)

            gate_high(0)
            xT_high(0)
            for c in range(1, KC):
                gate_high(c)
            for c in range(KC):
                act.wait_ge(up_loaded[c], 16)
                high_part(up_hi[:, c, :], up_raw[:, c, :]).then_inc(up_hi_ready, 1)

            def down_high():
                act.wait_ge(down_loaded, 32)
                for c0, c1 in ((0, 5), (5, BLOCKS - 1)):
                    high_part(down_hi[:, c0:c1, :], down_raw[:, c0:c1, :]).then_inc(down_hi_ready, 1)
                high_part(down_hi[0:LAST, BLOCKS - 1, :], down_raw[0:LAST, BLOCKS - 1, :]).then_inc(down_hi_ready, 1)

            def iteration(i, b, has):
                first = isinstance(i, int) and i == 0

                def count(k):
                    act.wait_ge(thr_ready, i * COUNTS + k + 1)
                    nc.scalar.activation(signs[:, :], mag[:, b, 0:INNER + PADS], ACT.Sign, bias=thr[:, :],
                                         scale=-1.0, accum_out=signed[:, :]).then_inc(counted, 1)

                def mT_high(g):
                    c0, cn = GROUPS[g]
                    act.wait_ge(mT_done, (i - 1) * NG + g + 1)
                    if g == 0:
                        wait(act, down_done, i - 1)
                    high_part(mT_hi[:, c0 * P:(c0 + cn) * P], ps_gate[:, c0 * P:(c0 + cn) * P]
                              ).then_inc(mT_hi_ready, 1)

                if has(0):
                    act.wait_ge(gate_done, i + 1)
                    wait(act, masked_ready, i - 1)
                    nc.scalar.activation(gated[:, b, :], ps_gate[:, 0:INNER], ACT.Silu).then_inc(silu_ready, 1)
                    if first:
                        act.wait_ge(consts_ready, 1)
                    act.wait_ge(silu_ready, i + 1)
                    nc.scalar.activation(mag[:, b, 0:INNER], gated[:, b, :], ACT.Abs,
                                         accum_out=mag_sum[:, :]).then_inc(mag_ready, 1)
                    if first:
                        down_high()
                    count(0)
                if has(-2):
                    act.wait_ge(x2T_done, i - 1)
                    high_part(x2T_hi[:, :], ps_x[:, :]).then_inc(x2T_hi_ready, 1)
                if has(0):
                    count(1)
                if has(1):
                    xT_high(i + 1)
                if has(-1):
                    mT_high(0)
                if has(0):
                    count(2)
                if has(-1):
                    mT_high(1)
                if has(0):
                    count(3)
                if has(-1):
                    mT_high(2)
                if has(0):
                    count(4)
                    count(5)
                if first:
                    act.wait_ge(lin_scaled, 1)
                    high_part(lin_hi[:, :, :], lin_raw).then_inc(lin_hi_ready, 1)

            assert NG == 3 and COUNTS == 6
            each_iteration(act, iteration)

        @block.vector
        def _(dve):
            V = nc.vector
            for b in range(2):
                V.memset(mag[:, b, INNER:INNER + WINDOW], 3e38)
            V.memset(ones[:, :], 1.0)
            for k, gain in enumerate(GAINS):
                V.memset(step_unit[:, k:k + 1], -gain * SPACING_PER_MEAN / INNER / 2)
            for r in range(WINDOW):
                V.memset(slot_of[:, r:r + 1], float(2 * r - PADS))
            V.memset(ps_gate[:, INNER:3 * BANK], 0.0).then_inc(consts_ready, 1)

            def take_stats(ln, src):
                V.bn_stats(ln.parts[:, :], src)
                dve.drain()
                V.bn_aggr(ln.mean_var[:, :], ln.parts[:, :]).then_inc(ln.taken, 1)

            def normalise(dst, src, ln, n):
                dve.wait_ge(ln.ready, n + 1)
                return V.tensor_scalar(dst, src, ln.mean_var[:, 0:1], ln.rstd[:, :], ALU.subtract, ALU.mult)

            def low_part(lo, src, hi):
                return V.tensor_tensor(lo, src, hi.bitcast(F32), ALU.subtract)

            def stats_in(n, b):
                dve.wait_ge(x_in_loaded[b], (n - b) * 8 + 16)
                take_stats(ln_in, x_in[:, b, :])

            def x_hat(n, b):
                normalise(x_in[:, b, :], x_in[:, b, :], ln_in, n).then_inc(x_hat_ready, 1)

            def xT_low(n):
                dve.wait_ge(xT_hi_ready, n + 1)
                low_part(xT_lo[:, :], ps_x[:, :], xT_hi[:, :]).then_inc(xT_lo_ready, 1)

            def exact_search(b):
                a = mag[:, b, 0:INNER]
                scratch = masked[:, :].bitcast(BF16)[:, 0:INNER]
                value = exact[:, :].bitcast(F32)
                V.memset(exact[:, :], 0)
                V.memset(bit[:, :], 1 << 30)
                dve.drain()
                with dve.Fori(0, 31):
                    V.tensor_tensor(trial[:, :], exact[:, :], bit[:, :], ALU.bitwise_or)
                    dve.drain()
                    V.tensor_scalar(scratch, a, trial[:, :].bitcast(F32), None, ALU.is_ge, ALU.add,
                                    accum_out=at_least[:, :])
                    V.tensor_scalar(bit[:, :], bit[:, :], 1, None, ALU.logical_shift_right)
                    dve.drain()
                    V.tensor_scalar(moves[:, :], at_least[:, :], float(INNER - DROP + 1), None, ALU.is_ge)
                    dve.drain()
                    V.copy_predicated(exact[:, :], moves[:, :], trial[:, :])
                    dve.drain()
                V.tensor_scalar(scratch, a, value, None, ALU.is_ge, ALU.add, accum_out=at_least[:, :])
                V.memset(carry[:, :], 0.0)
                dve.drain()
                V.tensor_scalar(at_least[:, :], at_least[:, :], float(INNER - DROP), None, ALU.subtract)
                V.tensor_scalar(masked[:, :], a, value, None, ALU.is_equal)
                dve.drain()
                for c0, cn in BANKS:
                    equal, kept, number = masked[:, c0:c0 + cn], mag[:, b, c0:c0 + cn], normed[:, 0:cn]
                    V.tensor_tensor_scan(number, equal, equal, carry[:, :], ALU.add, ALU.max)
                    dve.drain()
                    V.tensor_copy(carry[:, :], normed[:, cn - 1:cn])
                    V.tensor_tensor(equal, number, equal, ALU.mult)
                    dve.drain()
                    V.tensor_scalar(equal, equal, at_least[:, :], None, ALU.is_gt)
                    dve.drain()
                    V.scalar_tensor_tensor(kept, kept, value, equal, ALU.is_gt, ALU.add)
                    dve.drain()
                V.memset(drop_at[:, :], 0.5)
                dve.drain()

            stats_in(0, 0)
            x_hat(0, 0)
            for c in range(KC):
                dve.wait_ge(gate_hi_ready, c + 1)
                low_part(gate_lo[:, c, :], gate_raw[:, c, :], gate_hi[:, c, :]).then_inc(gate_lo_ready, 1)
                if c == 0:
                    xT_low(0)
            for c in range(KC):
                dve.wait_ge(up_hi_ready, c + 1)
                low_part(up_lo[:, c, :], up_raw[:, c, :], up_hi[:, c, :]).then_inc(up_lo_ready, 1)

            def iteration(i, b, has):
                def start_threshold():
                    dve.wait_ge(mag_ready, i + 1)
                    V.tensor_scalar(step[:, :], step_unit[:, :], mag_sum[:, :], None, ALU.mult)
                    V.tensor_scalar(thr[:, :], mag_sum[:, :], MEDIAN_PER_MEAN / INNER, None,
                                    ALU.mult).then_inc(thr_ready, 1)

                def move_threshold(k):
                    dve.wait_ge(counted, i * COUNTS + k + 1)
                    V.tensor_scalar(moves[:, :], signed[:, :], signed[:, :], (PADS + 0.5) ** 2, ALU.mult, ALU.is_gt)
                    V.scalar_tensor_tensor(thr_new[:, :], signed[:, :], step[:, k:k + 1], thr[:, :],
                                           ALU.mult, ALU.add)
                    dve.drain()
                    V.copy_predicated(thr[:, :], moves[:, :], thr_new[:, :]).then_inc(thr_ready, 1)

                def mT_low(g):
                    c0, cn = GROUPS[g]
                    cols = slice(c0 * P, (c0 + cn) * P)
                    dve.wait_ge(mT_hi_ready, (i - 1) * NG + g + 1)
                    low_part(mT_lo[:, cols], ps_gate[:, cols], mT_hi[:, cols]).then_inc(mT_lo_ready, 1)

                if has(-1):
                    dve.wait_ge(counted, i * COUNTS)
                    wait(dve, mT_done, (i - 1) * NG)
                    V.tensor_copy(top[:, 0:1], thr[:, :])
                    V.scalar_tensor_tensor(masked[:, :], mag[:, 1 - b, 0:INNER], thr[:, :], mag[:, 1 - b, 0:INNER],
                                           ALU.is_le, ALU.mult)
                if has(-2):
                    dve.wait_ge(down_done, i - 1)
                    take_stats(ln_mlp, ps_down[:, :])
                if has(-1):
                    dve.drain()
                    V.max(top[:, 1:], masked[:, :])
                if has(-2):
                    wait(dve, out_ready, i - 2)
                    normalise(normed[:, :], ps_down[:, :], ln_mlp, i - 2).then_inc(down_read, 1)
                if has(-1):
                    dve.drain()
                    V.scalar_tensor_tensor(pick[:, 0, :], slot_of[:, :], signed[:, :], top[:, 1:], ALU.is_equal,
                                           ALU.mult, accum_out=drop_at[:, :])
                    V.scalar_tensor_tensor(pick[:, 1, :], slot_of[:, :], signed[:, :], top[:, 0:WINDOW], ALU.is_equal,
                                           ALU.mult, accum_out=above[:, :])
                if has(-2):
                    if not has(-1):
                        dve.drain()
                    dve.wait_ge(x_res_loaded[b], (i - b) * 8)
                    V.tensor_tensor(x_res[:, b, :], x_res[:, b, :], normed[:, :], ALU.add)
                if has(-1):
                    dve.drain()
                    V.tensor_tensor(tied[:, :], drop_at[:, :], above[:, :], ALU.is_ge)
                    dve.drain()
                    V.scalar_tensor_tensor(bad[:, :], top[:, 1:2], thr[:, :], tied[:, :], ALU.is_ge,
                                           ALU.add).then_inc(bad_ready, 1)
                if has(-2):
                    dve.drain()
                    take_stats(ln_mid, x_res[:, b, :])
                if has(1):
                    stats_in(i + 1, 1 - b)
                if has(-2):
                    wait(dve, x2T_done, i - 2)
                    normalise(x2_hat[:, :], x_res[:, b, :], ln_mid, i - 2).then_inc(x2_hat_ready, 1)
                if has(1):
                    x_hat(i + 1, 1 - b)
                if has(0):
                    start_threshold()
                if has(-1):
                    dve.wait_ge(flag_done, i)
                    V.tensor_copy(bad_rows[:, :], flag_sum)
                    dve.drain()
                    rows = dve.value_load(bad_rows[0:1, 0:1], min_val=0, max_val=2 * P)
                    with dve.If(rows > 0):
                        exact_search(1 - b)
                    V.scalar_tensor_tensor(masked[:, :], mag[:, 1 - b, 0:INNER], drop_at[:, :], gated[:, 1 - b, :],
                                           ALU.is_gt, ALU.mult).then_inc(masked_ready, 1)
                if has(0):
                    move_threshold(0)
                if has(-2):
                    dve.wait_ge(x2T_hi_ready, i - 1)
                    low_part(x2T_lo[:, :], ps_x[:, :], x2T_hi[:, :]).then_inc(x2T_lo_ready, 1)
                if has(0):
                    move_threshold(1)
                if has(1):
                    xT_low(i + 1)
                if has(-1):
                    mT_low(0)
                if has(0):
                    move_threshold(2)
                if has(-1):
                    mT_low(1)
                if has(0):
                    dve.wait_ge(up_done, i + 1)
                    V.tensor_tensor(gated[:, b, :], gated[:, b, :], ps_up[:, 0:INNER],
                                    ALU.mult).then_inc(product_ready, 1)
                    move_threshold(3)
                if has(-1):
                    mT_low(2)
                if has(-2):
                    dve.wait_ge(lin_done, i - 1)
                    take_stats(ln_lin, ps_x[:, :])
                if has(0):
                    move_threshold(4)
                if has(-2):
                    normalise(normed[:, :], ps_x[:, :], ln_lin, i - 2).then_inc(lin_read, 1)

            each_iteration(dve, iteration)

        @block.tensor
        def _(pe):
            def product(dst, lhs_hi, lhs_lo, rhs_hi, rhs_lo, first, last):
                nc.tensor.matmul(dst, lhs_hi, rhs_hi, start=first, stop=False)
                nc.tensor.matmul(dst, lhs_hi, rhs_lo, start=False, stop=False)
                return nc.tensor.matmul(dst, lhs_lo, rhs_hi, start=False, stop=last)

            def transpose_rows(dst, src):
                for c in range(KC):
                    last = nc.tensor.transpose(dst[:, c * P:(c + 1) * P], src[:, c * P:(c + 1) * P], ident[:, :])
                return last

            def xT(n, b):
                pe.wait_ge(x_hat_ready, n + 1)
                transpose_rows(ps_x, x_in[:, b, :]).then_inc(xT_done, 1)

            def wide(dst, w_hi, w_lo, c):
                k = slice(c * P, (c + 1) * P)
                for c0, cn in BANKS:
                    cols = slice(c0, c0 + cn)
                    last = product(dst[:, cols], xT_hi[:, k], xT_lo[:, k], w_hi[:, c, cols], w_lo[:, c, cols],
                                   c == 0, c == KC - 1)
                return last

            pe.wait_ge(ident_ready, 1)
            xT(0, 0)

            def iteration(i, b, has):
                first = isinstance(i, int) and i == 0
                if has(0):
                    pe.wait_ge(xT_hi_ready, i + 1)
                    pe.wait_ge(xT_lo_ready, i + 1)
                    wait(pe, mT_lo_ready, (i - 1) * NG)
                    if first:
                        pe.wait_ge(consts_ready, 1)
                    for c in range(KC):
                        if first:
                            pe.wait_ge(gate_hi_ready, c + 1)
                            pe.wait_ge(gate_lo_ready, c + 1)
                        last = wide(ps_gate, gate_hi, gate_lo, c)
                    last.then_inc(gate_done, 1)
                    wait(pe, product_ready, i)

                def up(c):
                    if first:
                        pe.wait_ge(up_hi_ready, c + 1)
                        pe.wait_ge(up_lo_ready, c + 1)
                    return wide(ps_up, up_hi, up_lo, c)

                if has(0):
                    up(0)
                    pe.wait_ge(silu_ready, i + 1)
                if has(-1):
                    pe.wait_ge(bad_ready, i)
                    nc.tensor.matmul(flag_sum, bad[:, :], ones[:, :], start=True, stop=True).then_inc(flag_done, 1)
                if has(0):
                    up(1)
                if has(-2):
                    pe.wait_ge(x2_hat_ready, i - 1)
                    wait(pe, lin_read, i - 2)
                    transpose_rows(ps_x, x2_hat).then_inc(x2T_done, 1)
                if has(0):
                    for c in range(2, KC):
                        last = up(c)
                    last.then_inc(up_done, 1)
                if has(1):
                    if has(-2):
                        pe.wait_ge(x2T_lo_ready, i - 1)
                    elif first:
                        pe.wait_ge(xT_lo_ready, 1)
                    xT(i + 1, 1 - b)
                if has(-1):
                    pe.wait_ge(masked_ready, i)
                    for c0, cn in GROUPS:
                        for c in range(c0, c0 + cn):
                            rows = min(P, INNER - c * P)
                            last = nc.tensor.transpose(ps_gate[0:rows, c * P:(c + 1) * P],
                                                       masked[:, c * P:c * P + rows], ident[:, :])
                        last.then_inc(mT_done, 1)
                if has(-2):
                    if has(1):
                        pe.wait_ge(xT_lo_ready, i + 2)
                    pe.wait_ge(x2T_hi_ready, i - 1)
                    pe.wait_ge(x2T_lo_ready, i - 1)
                    if isinstance(i, int) and i == 2:
                        pe.wait_ge(lin_hi_ready, 1)
                        pe.wait_ge(lin_lo_ready, 1)
                    for c in range(KC):
                        k = slice(c * P, (c + 1) * P)
                        last = product(ps_x[:, :], x2T_hi[:, k], x2T_lo[:, k], lin_hi[:, c, :], lin_lo[:, c, :],
                                       c == 0, c == KC - 1)
                    last.then_inc(lin_done, 1)
                if has(-1):
                    wait(pe, down_read, i - 1)
                    if isinstance(i, int) and i == 1:
                        pe.wait_ge(down_hi_ready, 3)
                        pe.wait_ge(down_lo_ready, 1)
                        pe.wait_ge(lin_hi_ready, 1)
                        pe.wait_ge(lin_lo_ready, 1)
                    for g, (c0, cn) in enumerate(GROUPS):
                        pe.wait_ge(mT_hi_ready, (i - 1) * NG + g + 1)
                        pe.wait_ge(mT_lo_ready, (i - 1) * NG + g + 1)
                        for c in range(c0, c0 + cn):
                            rows = min(P, INNER - c * P)
                            k = slice(c * P, (c + 1) * P)
                            last = product(ps_down[:, :], mT_hi[0:rows, k], mT_lo[0:rows, k],
                                           down_hi[0:rows, c, :], down_lo[0:rows, c, :], c == 0, c == BLOCKS - 1)
                    last.then_inc(down_done, 1)

            each_iteration(pe, iteration)


def kernel(L0_attn_x, L0_attn_w_gate, L0_attn_w_up, L0_attn_w_down, L0_ffn_weight, L0_ffn_weight_scale):
    import numpy as np
    import concourse.bacc as bacc
    from concourse.bass_utils import run_bass_kernel_spmd

    nc = bacc.Bacc("TRN2", target_bir_lowering=False, num_devices=1)
    x = np.asarray(L0_attn_x)
    arrays = {
        "x": x.reshape(-1, x.shape[-1]),
        "w_gate_t": np.ascontiguousarray(np.asarray(L0_attn_w_gate).T),
        "w_up_t": np.ascontiguousarray(np.asarray(L0_attn_w_up).T),
        "w_down_t": np.ascontiguousarray(np.asarray(L0_attn_w_down).T),
        "w_lin_t": np.ascontiguousarray(np.asarray(L0_ffn_weight).T),
        "lin_scale_t": np.ascontiguousarray(np.asarray(L0_ffn_weight_scale).T).reshape(-1),
    }
    aps = [nc.dram_tensor(n + "_dram", a.shape, mybir.dt.from_np(a.dtype), kind="ExternalInput").ap()
           for n, a in arrays.items()]
    out = nc.dram_tensor("out_dram", arrays["x"].shape, F32, kind="ExternalOutput").ap()
    sandwich_kernel(nc, *aps, out)
    r = run_bass_kernel_spmd(nc, [{n + "_dram": a for n, a in arrays.items()}], core_ids=[0])
    return r.results[0]["out_dram"].reshape(x.shape)
```

```python
from contextlib import ExitStack

import concourse.bass as bass
from concourse import mybir

ALU = mybir.AluOpType
ACT = mybir.ActivationFunctionType
F32 = mybir.dt.float32
F32R = mybir.dt.float32r
BF16 = mybir.dt.bfloat16
I32 = mybir.dt.int32
I8 = mybir.dt.int8

P = 128
BANK = 512
EPS = 1e-5

MEDIAN_PER_MEAN = 0.8145
SPACING_PER_MEAN = 1.2666e-3
GAINS = (1.0, 0.8, 0.5, 0.4, 0.25, 0.3)
COUNTS = len(GAINS) + 1
WINDOW = 8


def sandwich_kernel(nc: bass.Bass, x: bass.AP, w_gate_t: bass.AP, w_up_t: bass.AP, w_down_t: bass.AP,
                    w_lin_t: bass.AP, lin_scale_t: bass.AP, out: bass.AP):
    TOKENS, H = x.shape
    INNER = w_gate_t.shape[1]
    TILES = TOKENS // P
    KC = H // P
    DROP = INNER // 2
    BLOCKS = -(-INNER // P)
    LAST = INNER - (BLOCKS - 1) * P
    BANKS = [(b, min(BANK, INNER - b)) for b in range(0, INNER, BANK)]
    GROUPS = [(b, min(4, BLOCKS - b)) for b in range(0, BLOCKS, 4)]
    NG = len(GROUPS)
    DOWN_LOAD = 2
    PADS = WINDOW - 1
    assert (BLOCKS - 1) % DOWN_LOAD == 0
    assert H == BANK and LAST % 32 == 0 and INNER % 2 == 0 and TILES % 2 == 0 and TILES >= 8

    x_tiles = x.rearrange("(n p) h -> n p h", p=P)
    out_tiles = out.rearrange("(n p) h -> n p h", p=P)

    with ExitStack() as ctx:
        def sb(name, shape, dt):
            return ctx.enter_context(nc.sbuf_tensor(name, shape, dt))

        def ps(name, width):
            return ctx.enter_context(nc.psum_tensor(name, [P, width], F32))

        def sem(name):
            return ctx.enter_context(nc.semaphore(name))

        low_at = -(-nc.sbuf_base // 32) * 32
        low_size = (2 * KC * INNER + BLOCKS * H + KC * H)
        weights_low = sb("weights_low", [P, low_size], F32)
        taken = [0]

        def raw_and_low(name, shape):
            words = shape[1] * shape[2]
            raw = weights_low[:, taken[0]:taken[0] + words].rearrange("p (c n) -> p c n", c=shape[1])
            low = nc.alloc_sbuf_tensor_at(name + "_lo", shape, F32R, offset=low_at + 4 * taken[0])
            taken[0] += words
            return raw, low

        gate_raw, gate_lo = raw_and_low("gate", [P, KC, INNER])
        up_raw, up_lo = raw_and_low("up", [P, KC, INNER])
        down_raw, down_lo = raw_and_low("down", [P, BLOCKS, H])
        lin_raw, lin_lo = raw_and_low("lin", [P, KC, H])
        gate_hi = sb("gate_hi", [P, KC, INNER], F32R)
        up_hi = sb("up_hi", [P, KC, INNER], F32R)
        down_hi = sb("down_hi", [P, BLOCKS, H], F32R)
        lin_hi = sb("lin_hi", [P, KC, H], F32R)
        lin_scale = sb("lin_scale", [P, KC * KC], F32)

        x_in = sb("x_in", [P, 2, H], F32)
        x_res = sb("x_res", [P, 2, H], F32)
        xT_hi = sb("xT_hi", [P, H], F32R)
        xT_lo = sb("xT_lo", [P, H], F32R)
        gated = sb("gated", [P, 2, INNER], F32)
        mag = sb("mag", [P, 2, INNER + WINDOW], F32)
        signs = sb("signs", [P, INNER + PADS], I8)
        masked = sb("masked", [P, INNER], F32)
        mT_hi = sb("mT_hi", [P, BLOCKS * P], F32R)
        mT_lo = sb("mT_lo", [P, BLOCKS * P], F32R)
        normed = sb("normed", [P, H], F32)
        x2_hat = sb("x2_hat", [P, H], F32)
        x2T_hi = sb("x2T_hi", [P, H], F32R)
        x2T_lo = sb("x2T_lo", [P, H], F32R)
        ident = sb("ident", [P, P], F32)
        ones = sb("ones", [P, 1], F32)
        busy = sb("busy", [P, 2 * P], BF16)
        unread = sb("unread", [P, 2], F32)
        eps_col = sb("eps_col", [P, 1], F32)
        neg_half = sb("neg_half", [P, 1], F32)

        thr = sb("thr", [P, 1], F32)
        thr_new = sb("thr_new", [P, 1], F32)
        moves = sb("moves", [P, 1], I32)
        mag_sum = sb("mag_sum", [P, 1], F32)
        step_unit = sb("step_unit", [P, len(GAINS)], F32)
        step = sb("step", [P, len(GAINS)], F32)
        signed = sb("signed", [P, 1], F32)
        slot_of = sb("slot_of", [P, WINDOW], F32)
        top = sb("top", [P, 1 + WINDOW], F32)
        at_thr = sb("at_thr", [P, 1], F32)
        slot = sb("slot", [P, 1], F32)
        pick = sb("pick", [P, 2, WINDOW], F32)
        drop_at = sb("drop_at", [P, 1], F32)
        above = sb("above", [P, 1], F32)
        full = sb("full", [P, 1], F32)
        bad = sb("bad", [P, 2], F32)
        bad_rows = sb("bad_rows", [1, 2], I32)
        exact = sb("exact", [P, 1], I32)
        trial = sb("trial", [P, 1], I32)
        bit = sb("bit", [P, 1], I32)
        at_least = sb("at_least", [P, 1], F32)
        carry = sb("carry", [P, 1], F32)

        class Stats:

            def __init__(self, name):
                self.parts = sb(name + "_parts", [P, 6], F32)
                self.mean_var = sb(name + "_mean_var", [P, 2], F32)
                self.var_eps = sb(name + "_var_eps", [P, 1], F32)
                self.rstd = sb(name + "_rstd", [P, 1], F32)
                self.taken = sem(name + "_stats_taken")
                self.ready = sem(name + "_rstd_ready")

        ln_in, ln_mlp, ln_mid, ln_lin = (Stats("ln_" + n) for n in ("in", "mlp", "mid", "lin"))

        ps_gate = ps("ps_gate", 3 * BANK)
        ps_up = ps("ps_up", 3 * BANK)
        ps_lin = ps("ps_lin", BANK)
        ps_down = ps("ps_down", BANK)
        FLAG = 3 * BANK - 2
        flag_sum = ps_gate[0:1, FLAG:FLAG + 2]

        gate_loaded = [sem(f"gate_loaded{c}") for c in range(KC)]
        up_loaded = [sem(f"up_loaded{c}") for c in range(KC)]
        down_loaded = [sem(f"down_loaded{n}") for n in range((BLOCKS - 1) // DOWN_LOAD + 1)]
        lin_loaded = sem("lin_loaded")
        x_in_loaded = [sem(f"x_in_loaded{b}") for b in range(2)]
        x_res_loaded = [sem(f"x_res_loaded{b}") for b in range(2)]
        out_stored = [sem(f"out_stored{b}") for b in range(2)]
        gate_hi_ready, gate_lo_ready = sem("gate_hi_ready"), sem("gate_lo_ready")
        up_hi_ready, up_lo_ready = sem("up_hi_ready"), sem("up_lo_ready")
        down_hi_ready, down_lo_ready = sem("down_hi_ready"), sem("down_lo_ready")
        lin_scaled, lin_hi_ready, lin_lo_ready = sem("lin_scaled"), sem("lin_hi_ready"), sem("lin_lo_ready")
        pool_set, ident_ready, consts_ready = sem("pool_set"), sem("ident_ready"), sem("consts_ready")
        x_hat_ready = sem("x_hat_ready")
        xT_done, xT_hi_ready, xT_lo_ready = sem("xT_done"), sem("xT_hi_ready"), sem("xT_lo_ready")
        gate_done, up_done = sem("gate_done"), sem("up_done")
        silu_ready, mag_ready = sem("silu_ready"), sem("mag_ready")
        thr_ready, counted = sem("thr_ready"), sem("counted")
        bad_ready, flag_done = sem("bad_ready"), sem("flag_done")
        product_ready, masked_ready = sem("product_ready"), sem("masked_ready")
        mT_done, mT_hi_ready, mT_lo_ready = sem("mT_done"), sem("mT_hi_ready"), sem("mT_lo_ready")
        down_done, down_read = sem("down_done"), sem("down_read")
        x2_hat_ready = sem("x2_hat_ready")
        x2T_done, x2T_hi_ready, x2T_lo_ready = sem("x2T_done"), sem("x2T_hi_ready"), sem("x2T_lo_ready")
        lin_done, lin_read, out_ready = sem("lin_done"), sem("lin_read"), sem("out_ready")

        def each_iteration(eng, iteration):
            def known(i):
                iteration(i, i % 2, lambda d: 0 <= i + d < TILES)
            for i in range(4):
                known(i)
            with eng.Fori(2, TILES // 2 - 1) as pair:
                for b in range(2):
                    iteration(pair * 2 + b, b, lambda d: True)
            for i in range(TILES - 2, TILES + 2):
                known(i)

        EARLY_DOWN = COUNTS - 1

        def is_number(i):
            return isinstance(i, int)

        def is_first(i):
            return is_number(i) and i == 0

        def is_second(i):
            return is_number(i) and i == 1

        def ramp(i):
            return is_first(i) or is_second(i)

        def is_tail(i):
            return is_number(i) and i == TILES

        def is_last(i):
            return is_number(i) and i == TILES + 1

        def down_bank(n):
            return ps_up[:, BANK:BANK + H] if is_number(n) and n == TILES - 1 else ps_down[:, :]

        def x2T_bank(n):
            return ps_up[:, 0:H] if is_number(n) and n == TILES - 1 else ps_lin[:, :]

        def wait(eng, semaphore, value):
            if not isinstance(value, int) or value > 0:
                eng.wait_ge(semaphore, value)

        block = ctx.enter_context(nc.Block())

        @block.sync
        def _(sp):
            def load_x_in(n, b):
                sp.dma_start(x_in[:, b, :], x_tiles[n]).then_inc(x_in_loaded[b], 16)

            def load_x_res(n, b):
                sp.dma_start(x_res[:, b, :], x_tiles[n]).then_inc(x_res_loaded[b], 16)

            load_x_in(0, 0)
            for c in range(KC):
                sp.dma_start(gate_raw[:, c, :], w_gate_t[c * P:(c + 1) * P, :]).then_inc(gate_loaded[c], 16)
            load_x_in(1, 1)
            for c in range(KC):
                sp.dma_start(up_raw[:, c, :], w_up_t[c * P:(c + 1) * P, :]).then_inc(up_loaded[c], 16)
            full = (BLOCKS - 1) * P
            for n, c0 in enumerate(range(0, BLOCKS - 1, DOWN_LOAD)):
                c1 = min(c0 + DOWN_LOAD, BLOCKS - 1)
                sp.dma_start(down_raw[:, c0:c1, :],
                             w_down_t[c0 * P:c1 * P, :].rearrange("(c p) h -> p c h", p=P)
                             ).then_inc(down_loaded[n], 16)
            sp.dma_start(down_raw[0:LAST, BLOCKS - 1, :], w_down_t[full:INNER, :]).then_inc(down_loaded[-1], 16)
            sp.wait_ge(xT_done, 1)
            load_x_in(2, 0)
            load_x_res(0, 0)
            load_x_res(1, 1)
            sp.dma_start(lin_scale[:, :], lin_scale_t.rearrange("(o n) -> o n", o=1).to_broadcast([P, KC * KC])
                         ).then_inc(lin_loaded, 16)
            sp.dma_start(lin_raw[:, :, :], w_lin_t.rearrange("(c p) h -> p c h", p=P)).then_inc(lin_loaded, 16)

            def iteration(i, b, has):
                if has(2) and not is_first(i):
                    sp.wait_ge(xT_done, i + 1)
                    load_x_in(i + 2, b)
                if has(-2):
                    sp.wait_ge(out_ready, i - 1)
                    sp.dma_start(out_tiles[i - 2], x_res[:, b, :]).then_inc(out_stored[b], 16)
                    if has(0):
                        sp.wait_ge(out_stored[b], (i - b) * 8)
                        load_x_res(i, b)

            each_iteration(sp, iteration)
            for b in range(2):
                sp.wait_ge(out_stored[b], 16 * (TILES // 2))

        @block.gpsimd
        def _(pool):
            nc.gpsimd.memset(ident[:, :], 0.0).then_inc(pool_set, 1)
            nc.gpsimd.memset(eps_col[:, :], EPS).then_inc(pool_set, 1)
            nc.gpsimd.memset(neg_half[:, :], -0.5).then_inc(pool_set, 1)
            pool.wait_ge(pool_set, 3)
            nc.gpsimd.affine_select(out=ident[:, :], in_=ident[:, :], compare_op=ALU.not_equal, fill=1.0, base=0,
                                    pattern=[[-1, P]], channel_multiplier=1).then_inc(ident_ready, 1)

            def rstd(ln, n):
                pool.wait_ge(ln.taken, n + 1)
                nc.gpsimd.tensor_tensor(ln.var_eps[:, :], ln.mean_var[:, 1:2], eps_col[:, :], ALU.add)
                pool.drain()
                nc.gpsimd.tensor_tensor(ln.rstd[:, :], ln.var_eps[:, :], neg_half[:, :], ALU.pow).then_inc(ln.ready, 1)

            def low_part(lo, raw, hi):
                return nc.gpsimd.tensor_tensor(lo, raw, hi.bitcast(F32), ALU.subtract)

            def second_residual(n, b):
                pool.wait_ge(lin_read, n + 1)
                nc.gpsimd.tensor_tensor(x_res[:, b, :], x_res[:, b, :], normed[:, :], ALU.add).then_inc(out_ready, 1)

            def iteration(i, b, has):
                if is_first(i):
                    down_low(range(EARLY_DOWN - 1))
                if is_second(i):
                    down_low(range(EARLY_DOWN, BLOCKS))
                    scale_lin()
                if has(-2):
                    rstd(ln_mlp, i - 2)
                    rstd(ln_mid, i - 2)
                if is_number(i) and i == 2:
                    lin_low()
                if has(0) and has(-2):
                    rstd(ln_lin, i - 2)
                if has(2):
                    rstd(ln_in, i + 2)
                if is_first(i):
                    down_low(range(EARLY_DOWN - 1, EARLY_DOWN))
                if has(0) and has(-2):
                    second_residual(i - 2, b)
                if is_last(i):
                    rstd(ln_lin, i - 3)
                    second_residual(i - 3, 1 - b)
                    rstd(ln_lin, i - 2)

            rstd(ln_in, 0)
            rstd(ln_in, 1)

            def down_low(blocks):
                for c in blocks:
                    rows = min(P, INNER - c * P)
                    pool.wait_ge(down_hi_ready, c + 1)
                    low_part(down_lo[0:rows, c, :], down_raw[0:rows, c, :],
                             down_hi[0:rows, c, :]).then_inc(down_lo_ready, 1)

            def scale_lin():
                pool.wait_ge(lin_loaded, 32)
                lin_blocks = lin_raw.rearrange("p c (o n) -> p (c o) n", n=P)
                nc.gpsimd.tensor_tensor(lin_blocks, lin_blocks,
                                        lin_scale[:, :].unsqueeze(2).to_broadcast([P, KC * KC, P]),
                                        ALU.mult).then_inc(lin_scaled, 1)

            def lin_low():
                pool.wait_ge(lin_hi_ready, KC)
                low_part(lin_lo[:, :, :], lin_raw, lin_hi[:, :, :]).then_inc(lin_lo_ready, 1)

            each_iteration(pool, iteration)

        @block.scalar
        def _(act):
            def high_part(hi, src):
                return nc.scalar.activation(hi, src, ACT.Copy)

            def gate_high(c):
                act.wait_ge(gate_loaded[c], 16)
                high_part(gate_hi[:, c, :], gate_raw[:, c, :]).then_inc(gate_hi_ready, 1)

            def xT_high(n):
                act.wait_ge(xT_done, n + 1)
                high_part(xT_hi[:, :], ps_down[:, :]).then_inc(xT_hi_ready, 1)

            act.wait_ge(consts_ready, 1)
            nc.scalar.activation(unread[:, 1:2], ones[:, :], ACT.Silu)
            gate_high(0)
            xT_high(0)
            for c in range(1, KC):
                gate_high(c)

            def up_high(c):
                act.wait_ge(up_loaded[c], 16)
                high_part(up_hi[:, c, :], up_raw[:, c, :]).then_inc(up_hi_ready, 1)

            def down_high(c):
                rows = min(P, INNER - c * P)
                act.wait_ge(down_loaded[c // DOWN_LOAD], 16)
                high_part(down_hi[0:rows, c, :], down_raw[0:rows, c, :]).then_inc(down_hi_ready, 1)

            for c in range(KC - 1):
                up_high(c)

            def iteration(i, b, has):
                def count(k):
                    act.wait_ge(thr_ready, i * COUNTS + k + 1)
                    nc.scalar.activation(signs[:, :], mag[:, b, 0:INNER + PADS], ACT.Sign, bias=thr[:, :],
                                         scale=-1.0, accum_out=signed[:, :]).then_inc(counted, 1)

                def mT_high(g):
                    c0, cn = GROUPS[g]
                    act.wait_ge(mT_done, (i - 1) * NG + g + 1)
                    if g == 0:
                        wait(act, down_done, i - 1)
                    high_part(mT_hi[:, c0 * P:(c0 + cn) * P], ps_gate[:, c0 * P:(c0 + cn) * P]
                              ).then_inc(mT_hi_ready, 1)

                def x2T_high():
                    act.wait_ge(x2T_done, i - 1)
                    if is_last(i):
                        act.wait_ge(lin_done, i - 2)
                    high_part(x2T_hi[:, :], x2T_bank(i - 2)).then_inc(x2T_hi_ready, 1)

                if has(0):
                    act.wait_ge(gate_done, i + 1)
                    wait(act, masked_ready, i - 1)
                    nc.scalar.activation(gated[:, b, :], ps_gate[:, 0:INNER], ACT.Silu).then_inc(silu_ready, 1)
                    if is_first(i):
                        up_high(KC - 1)
                    act.wait_ge(silu_ready, i + 1)
                    nc.scalar.activation(mag[:, b, 0:INNER], gated[:, b, :], ACT.Abs,
                                         accum_out=mag_sum[:, :]).then_inc(mag_ready, 1)
                    if is_second(i):
                        for c in range(EARLY_DOWN, BLOCKS):
                            down_high(c)
                    count(0)
                if ramp(i):
                    xT_high(i + 1)
                if is_second(i):
                    mT_high(0)
                if has(-2) and not is_tail(i):
                    x2T_high()
                if has(0):
                    count(1)
                if is_first(i):
                    down_high(0)
                if has(1) and not ramp(i):
                    xT_high(i + 1)
                if has(-1) and not is_second(i):
                    mT_high(0)
                for k in range(2, COUNTS):
                    if has(0):
                        count(k)
                    if has(-1) and k - 1 < NG:
                        mT_high(k - 1)
                    if is_first(i):
                        down_high(k - 1)
                    if is_second(i) and k >= COUNTS - KC:
                        c = k - (COUNTS - KC)
                        act.wait_ge(lin_scaled, 1)
                        high_part(lin_hi[:, c, :], lin_raw[:, c, :]).then_inc(lin_hi_ready, 1)
                if is_tail(i):
                    x2T_high()

            assert NG < COUNTS and KC <= COUNTS - 2 and EARLY_DOWN <= BLOCKS
            each_iteration(act, iteration)

        @block.vector
        def _(dve):
            V = nc.vector
            for b in range(2):
                V.memset(mag[:, b, INNER:INNER + WINDOW], 3e38)
            V.memset(ones[:, :], 1.0)
            V.memset(busy[:, :], 1.0)
            for k, gain in enumerate(GAINS):
                V.memset(step_unit[:, k:k + 1], -gain * SPACING_PER_MEAN / INNER / 2)
            for r in range(WINDOW):
                V.memset(slot_of[:, r:r + 1], float(2 * r - PADS))
            V.memset(top[:, 0:1], 3e38)
            V.memset(ps_gate[:, INNER:3 * BANK], 0.0).then_inc(consts_ready, 1)

            def take_stats(ln, src):
                V.bn_stats(ln.parts[:, :], src)
                dve.drain()
                V.bn_aggr(ln.mean_var[:, :], ln.parts[:, :]).then_inc(ln.taken, 1)

            def normalise(dst, src, ln, n):
                dve.wait_ge(ln.ready, n + 1)
                return V.tensor_scalar(dst, src, ln.mean_var[:, 0:1], ln.rstd[:, :], ALU.subtract, ALU.mult)

            def low_part(lo, src, hi):
                return V.tensor_tensor(lo, src, hi.bitcast(F32), ALU.subtract)

            def stats_in(n, b):
                dve.wait_ge(x_in_loaded[b], (n - b) * 8 + 16)
                take_stats(ln_in, x_in[:, b, :])

            def x_hat(n, b):
                normalise(x_in[:, b, :], x_in[:, b, :], ln_in, n).then_inc(x_hat_ready, 1)

            def xT_low(n):
                dve.wait_ge(xT_hi_ready, n + 1)
                low_part(xT_lo[:, :], ps_down[:, :], xT_hi[:, :]).then_inc(xT_lo_ready, 1)

            def exact_search(b):
                a = mag[:, b, 0:INNER]
                scratch = masked[:, :].bitcast(BF16)[:, 0:INNER]
                value = exact[:, :].bitcast(F32)
                V.tensor_copy(value, drop_at[:, :])
                dve.drain()
                unsearched = dve.value_load(bad_rows[0:1, 1:2], min_val=0, max_val=2 * P)
                with dve.If(unsearched > 0):
                    V.memset(exact[:, :], 0)
                    V.memset(bit[:, :], 1 << 30)
                    dve.drain()
                    with dve.Fori(0, 31):
                        V.tensor_tensor(trial[:, :], exact[:, :], bit[:, :], ALU.bitwise_or)
                        dve.drain()
                        V.tensor_scalar(scratch, a, trial[:, :].bitcast(F32), None, ALU.is_ge, ALU.add,
                                        accum_out=at_least[:, :])
                        V.tensor_scalar(bit[:, :], bit[:, :], 1, None, ALU.logical_shift_right)
                        dve.drain()
                        V.tensor_scalar(moves[:, :], at_least[:, :], float(INNER - DROP + 1), None, ALU.is_ge)
                        dve.drain()
                        V.copy_predicated(exact[:, :], moves[:, :], trial[:, :])
                        dve.drain()
                dve.drain()
                V.tensor_scalar(scratch, a, value, None, ALU.is_ge, ALU.add, accum_out=at_least[:, :])
                V.memset(carry[:, :], 0.0)
                dve.drain()
                V.tensor_scalar(at_least[:, :], at_least[:, :], float(INNER - DROP), None, ALU.subtract)
                V.tensor_scalar(masked[:, :], a, value, None, ALU.is_equal)
                dve.drain()
                for c0, cn in BANKS:
                    equal, kept, number = masked[:, c0:c0 + cn], mag[:, b, c0:c0 + cn], normed[:, 0:cn]
                    V.tensor_tensor_scan(number, equal, equal, carry[:, :], ALU.add, ALU.max)
                    dve.drain()
                    V.tensor_copy(carry[:, :], normed[:, cn - 1:cn])
                    V.tensor_tensor(equal, number, equal, ALU.mult)
                    dve.drain()
                    V.tensor_scalar(equal, equal, at_least[:, :], None, ALU.is_gt)
                    dve.drain()
                    V.scalar_tensor_tensor(kept, kept, value, equal, ALU.is_gt, ALU.add)
                    dve.drain()
                V.memset(drop_at[:, :], 0.5)
                dve.drain()

            def up_low(c):
                dve.wait_ge(up_hi_ready, c + 1)
                low_part(up_lo[:, c, :], up_raw[:, c, :], up_hi[:, c, :]).then_inc(up_lo_ready, 1)

            stats_in(0, 0)
            x_hat(0, 0)
            for c in range(KC):
                dve.wait_ge(gate_hi_ready, c + 1)
                low_part(gate_lo[:, c, :], gate_raw[:, c, :], gate_hi[:, c, :]).then_inc(gate_lo_ready, 1)
                if c == 0:
                    xT_low(0)
            for c in range(KC - 1):
                up_low(c)
            stats_in(1, 1)
            up_low(KC - 1)
            x_hat(1, 1)

            def iteration(i, b, has):
                first = is_first(i)

                def start_threshold():
                    dve.wait_ge(mag_ready, i + 1)
                    V.tensor_scalar(step[:, :], step_unit[:, :], mag_sum[:, :], None, ALU.mult)
                    V.tensor_scalar(thr[:, :], mag_sum[:, :], MEDIAN_PER_MEAN / INNER, None,
                                    ALU.mult).then_inc(thr_ready, 1)

                def move_threshold(k):
                    dve.wait_ge(counted, i * COUNTS + k + 1)
                    V.tensor_scalar(moves[:, :], signed[:, :], signed[:, :], (PADS + 0.5) ** 2, ALU.mult, ALU.is_gt)
                    V.scalar_tensor_tensor(thr_new[:, :], signed[:, :], step[:, k:k + 1], thr[:, :],
                                           ALU.mult, ALU.add)
                    dve.drain()
                    V.copy_predicated(thr[:, :], moves[:, :], thr_new[:, :]).then_inc(thr_ready, 1)

                def mT_low(g):
                    c0, cn = GROUPS[g]
                    cols = slice(c0 * P, (c0 + cn) * P)
                    dve.wait_ge(mT_hi_ready, (i - 1) * NG + g + 1)
                    low_part(mT_lo[:, cols], ps_gate[:, cols], mT_hi[:, cols]).then_inc(mT_lo_ready, 1)

                def first_residual():
                    wait(dve, out_ready, i - 3 if is_last(i) else i - 2)
                    normalise(normed[:, :], down_bank(i - 2), ln_mlp, i - 2).then_inc(down_read, 1)
                    dve.drain()
                    dve.wait_ge(x_res_loaded[b], (i - b) * 8)
                    V.tensor_tensor(x_res[:, b, :], x_res[:, b, :], normed[:, :], ALU.add)

                def second_norm():
                    wait(dve, x2T_done, i - 2)
                    normalise(x2_hat[:, :], x_res[:, b, :], ln_mid, i - 2).then_inc(x2_hat_ready, 1)

                def x2T_low(n):
                    dve.wait_ge(x2T_hi_ready, n + 1)
                    low_part(x2T_lo[:, :], x2T_bank(n), x2T_hi[:, :]).then_inc(x2T_lo_ready, 1)

                def keep():
                    V.scalar_tensor_tensor(masked[:, :], mag[:, 1 - b, 0:INNER], drop_at[:, :], gated[:, 1 - b, :],
                                           ALU.is_gt, ALU.mult)

                def largest_below():
                    dve.drain()
                    wait(dve, mT_done, i * NG)
                    V.scalar_tensor_tensor(masked[:, :], mag[:, b, 0:INNER], thr[:, :], mag[:, b, 0:INNER],
                                           ALU.is_le, ALU.mult)
                    dve.drain()
                    V.max(top[:, 1:], masked[:, :])
                    dve.drain()
                    V.tensor_scalar(pick[:, 0, :], top[:, 1:], thr[:, :], None, ALU.is_equal, ALU.add,
                                    accum_out=at_thr[:, :])
                    V.tensor_tensor(full[:, :], top[:, WINDOW:], thr[:, :], ALU.is_ge)
                    dve.drain()

                def linear_stats(n):
                    dve.wait_ge(lin_done, n + 1)
                    take_stats(ln_lin, ps_lin[:, :])

                def down_stats():
                    dve.wait_ge(down_done, i - 1)
                    take_stats(ln_mlp, down_bank(i - 2))

                if has(-2) and not is_tail(i):
                    down_stats()
                if is_last(i):
                    x2T_low(i - 3)
                    first_residual()
                    dve.drain()
                    take_stats(ln_mid, x_res[:, b, :])
                    linear_stats(i - 3)
                    second_norm()
                    normalise(normed[:, :], ps_lin[:, :], ln_lin, i - 3).then_inc(lin_read, 1)
                    x2T_low(i - 2)
                    linear_stats(i - 2)
                    dve.wait_ge(out_ready, i - 2)
                    normalise(normed[:, :], ps_lin[:, :], ln_lin, i - 2)
                    dve.drain()
                    V.tensor_tensor(x_res[:, b, :], x_res[:, b, :], normed[:, :], ALU.add).then_inc(out_ready, 1)
                if has(-1):
                    dve.wait_ge(counted, i * COUNTS)
                    V.tensor_tensor(slot[:, :], signed[:, :], at_thr[:, :], ALU.add)
                    dve.drain()
                    V.scalar_tensor_tensor(pick[:, 0, :], slot_of[:, :], slot[:, :], top[:, 1:], ALU.is_equal,
                                           ALU.mult, accum_out=drop_at[:, :])
                    V.scalar_tensor_tensor(pick[:, 1, :], slot_of[:, :], slot[:, :], top[:, 0:WINDOW], ALU.is_equal,
                                           ALU.mult, accum_out=above[:, :])
                    dve.drain()
                    V.scalar_tensor_tensor(bad[:, 0:1], drop_at[:, :], above[:, :], full[:, :], ALU.is_ge, ALU.add)
                    V.scalar_tensor_tensor(bad[:, 1:2], above[:, :], 0.0, full[:, :], ALU.is_equal,
                                           ALU.add).then_inc(bad_ready, 1)
                if has(-2) and has(0):
                    first_residual()
                    dve.drain()
                    take_stats(ln_mid, x_res[:, b, :])
                if has(-1):
                    keep()
                if has(-2) and has(0):
                    second_norm()
                if has(0):
                    start_threshold()
                if has(-1):
                    if is_tail(i):
                        dve.wait_ge(out_ready, i - 2)
                    dve.wait_ge(flag_done, i)
                    V.tensor_copy(bad_rows[:, :], flag_sum)
                    dve.drain()
                    unsettled = dve.value_load(bad_rows[0:1, 0:1], min_val=0, max_val=2 * P)
                    with dve.If(unsettled > 0):
                        exact_search(1 - b)
                        keep()
                        dve.drain()
                    V.tensor_copy(unread[:, 0:1], ones[:, :]).then_inc(masked_ready, 1)
                if has(0):
                    move_threshold(0)
                if ramp(i):
                    xT_low(i + 1)
                if is_second(i):
                    mT_low(0)
                if has(-2) and has(0):
                    x2T_low(i - 2)
                if has(0):
                    move_threshold(1)
                if has(1) and not ramp(i):
                    xT_low(i + 1)
                if has(-1) and not is_second(i):
                    mT_low(0)
                if has(0):
                    move_threshold(2)
                if has(-1):
                    mT_low(1)
                if has(0):
                    dve.wait_ge(up_done, i + 1)
                    V.tensor_tensor(gated[:, b, :], gated[:, b, :], ps_up[:, 0:INNER],
                                    ALU.mult).then_inc(product_ready, 1)
                    move_threshold(3)
                if has(-1):
                    mT_low(2)
                if is_tail(i):
                    down_stats()
                    first_residual()
                    dve.drain()
                    take_stats(ln_mid, x_res[:, b, :])
                    second_norm()
                if has(-2) and has(0):
                    linear_stats(i - 2)
                if has(0):
                    move_threshold(4)
                if has(2):
                    stats_in(i + 2, b)
                if has(-2) and has(0):
                    normalise(normed[:, :], ps_lin[:, :], ln_lin, i - 2).then_inc(lin_read, 1)
                if has(0):
                    for k in range(5, len(GAINS)):
                        move_threshold(k)
                    largest_below()
                if has(2):
                    x_hat(i + 2, b)

            each_iteration(dve, iteration)

        @block.tensor
        def _(pe):
            def product(parts, lhs_hi, lhs_lo, first, last):
                for dst, rhs_hi, rhs_lo in parts:
                    nc.tensor.matmul(dst, lhs_hi, rhs_hi, start=first, stop=False)
                    nc.tensor.matmul(dst, lhs_hi, rhs_lo, start=False, stop=False)
                for dst, rhs_hi, _ in parts:
                    mm = nc.tensor.matmul(dst, lhs_lo, rhs_hi, start=False, stop=last)
                return mm

            def transpose_rows(dst, src):
                for c in range(KC):
                    last = nc.tensor.transpose(dst[:, c * P:(c + 1) * P], src[:, c * P:(c + 1) * P], ident[:, :])
                return last

            def xT(n, b):
                pe.wait_ge(x_hat_ready, n + 1)
                transpose_rows(ps_down, x_in[:, b, :]).then_inc(xT_done, 1)

            def wide(dst, w_hi, w_lo, c):
                k = slice(c * P, (c + 1) * P)
                cols = [slice(c0, c0 + cn) for c0, cn in BANKS]
                return product([(dst[:, s], w_hi[:, c, s], w_lo[:, c, s]) for s in cols],
                               xT_hi[:, k], xT_lo[:, k], c == 0, c == KC - 1)

            def keep_clock(matmuls):
                for _ in range(matmuls):
                    nc.tensor.matmul(ps_up[:, 2 * BANK:2 * BANK + 2 * P], busy[:, 0:P], busy[:, :], start=True, stop=True)

            pe.wait_ge(consts_ready, 1)
            keep_clock(15)
            pe.wait_ge(ident_ready, 1)
            xT(0, 0)
            keep_clock(22)

            def iteration(i, b, has):
                first = is_first(i)
                if has(0):
                    pe.wait_ge(xT_hi_ready, i + 1)
                    pe.wait_ge(xT_lo_ready, i + 1)
                    wait(pe, mT_lo_ready, (i - 1) * NG)
                    for c in range(KC):
                        if first:
                            pe.wait_ge(gate_hi_ready, c + 1)
                            pe.wait_ge(gate_lo_ready, c + 1)
                        last = wide(ps_gate, gate_hi, gate_lo, c)
                    last.then_inc(gate_done, 1)
                    wait(pe, product_ready, i)

                def up(c):
                    if first:
                        pe.wait_ge(up_hi_ready, c + 1)
                        pe.wait_ge(up_lo_ready, c + 1)
                    return wide(ps_up, up_hi, up_lo, c)

                def flag():
                    pe.wait_ge(bad_ready, i)
                    if has(0):
                        pe.wait_ge(silu_ready, i + 1)
                    nc.tensor.matmul(flag_sum, ones[:, :], bad[:, :], start=True, stop=True).then_inc(flag_done, 1)

                def linear():
                    pe.wait_ge(x2T_hi_ready, i - 1)
                    pe.wait_ge(x2T_lo_ready, i - 1)
                    if is_number(i) and i == 2:
                        pe.wait_ge(lin_hi_ready, KC)
                        pe.wait_ge(lin_lo_ready, 1)
                    for c in range(KC):
                        k = slice(c * P, (c + 1) * P)
                        last = product([(ps_lin[:, :], lin_hi[:, c, :], lin_lo[:, c, :])], x2T_hi[:, k], x2T_lo[:, k],
                                       c == 0, c == KC - 1)
                    last.then_inc(lin_done, 1)

                at_end = is_second(i)
                def transpose_second_norm():
                    pe.wait_ge(x2_hat_ready, i - 1)
                    if not is_last(i):
                        wait(pe, lin_read, i - 2)
                    transpose_rows(x2T_bank(i - 2), x2_hat).then_inc(x2T_done, 1)

                if has(0):
                    up(0)
                if is_tail(i):
                    pe.wait_ge(product_ready, TILES)
                    keep_clock(34)
                if has(-1) and not at_end:
                    flag()
                if is_tail(i):
                    keep_clock(24)
                if has(0):
                    up(1)
                if has(-2) and not is_tail(i):
                    transpose_second_norm()
                if is_last(i):
                    keep_clock(15)
                    pe.wait_ge(lin_read, i - 2)
                    linear()
                if has(0):
                    up(2)
                    up(3).then_inc(up_done, 1)
                if at_end:
                    flag()
                if has(1):
                    if first:
                        pe.wait_ge(xT_lo_ready, 1)
                    wait(pe, down_read, i - 1)
                    xT(i + 1, 1 - b)
                if has(-1):
                    pe.wait_ge(masked_ready, i)
                    for c0, cn in GROUPS:
                        for c in range(c0, c0 + cn):
                            rows = min(P, INNER - c * P)
                            last = nc.tensor.transpose(ps_gate[0:rows, c * P:(c + 1) * P],
                                                       masked[:, c * P:c * P + rows], ident[:, :])
                        last.then_inc(mT_done, 1)
                if has(-2) and has(0):
                    linear()
                if has(-1):
                    if has(1):
                        pe.wait_ge(xT_lo_ready, i + 2)
                    elif not is_tail(i):
                        pe.wait_ge(down_read, i - 1)
                    for g, (c0, cn) in enumerate(GROUPS):
                        pe.wait_ge(mT_hi_ready, (i - 1) * NG + g + 1)
                        pe.wait_ge(mT_lo_ready, (i - 1) * NG + g + 1)
                        for c in range(c0, c0 + cn):
                            rows = min(P, INNER - c * P)
                            k = slice(c * P, (c + 1) * P)
                            if is_second(i):
                                pe.wait_ge(down_hi_ready, c + 1)
                                pe.wait_ge(down_lo_ready, c + 1)
                            last = product([(down_bank(i - 1), down_hi[0:rows, c, :], down_lo[0:rows, c, :])],
                                           mT_hi[0:rows, k], mT_lo[0:rows, k], c == 0, c == BLOCKS - 1)
                    last.then_inc(down_done, 1)
                if is_tail(i):
                    transpose_second_norm()
                    linear()
                    keep_clock(31)

            each_iteration(pe, iteration)


def kernel(L0_attn_x, L0_attn_w_gate, L0_attn_w_up, L0_attn_w_down, L0_ffn_weight, L0_ffn_weight_scale):
    import numpy as np
    import concourse.bacc as bacc
    from concourse.bass_utils import run_bass_kernel_spmd

    nc = bacc.Bacc("TRN2", target_bir_lowering=False, num_devices=1)
    x = np.asarray(L0_attn_x)
    arrays = {
        "x": x.reshape(-1, x.shape[-1]),
        "w_gate_t": np.ascontiguousarray(np.asarray(L0_attn_w_gate).T),
        "w_up_t": np.ascontiguousarray(np.asarray(L0_attn_w_up).T),
        "w_down_t": np.ascontiguousarray(np.asarray(L0_attn_w_down).T),
        "w_lin_t": np.ascontiguousarray(np.asarray(L0_ffn_weight).T),
        "lin_scale_t": np.ascontiguousarray(np.asarray(L0_ffn_weight_scale).T).reshape(-1),
    }
    aps = [nc.dram_tensor(n + "_dram", a.shape, mybir.dt.from_np(a.dtype), kind="ExternalInput").ap()
           for n, a in arrays.items()]
    out = nc.dram_tensor("out_dram", arrays["x"].shape, F32, kind="ExternalOutput").ap()
    sandwich_kernel(nc, *aps, out)
    r = run_bass_kernel_spmd(nc, [{n + "_dram": a for n, a in arrays.items()}], core_ids=[0])
    return r.results[0]["out_dram"].reshape(x.shape)
```

```python
from contextlib import ExitStack

import concourse.bass as bass
from concourse import mybir

ALU = mybir.AluOpType
ACT = mybir.ActivationFunctionType
F32 = mybir.dt.float32
F32R = mybir.dt.float32r
BF16 = mybir.dt.bfloat16
I32 = mybir.dt.int32
I8 = mybir.dt.int8

P = 128
BANK = 512
EPS = 1e-5

MEDIAN_PER_MEAN = 0.8145
SPACING_PER_MEAN = 1.2666e-3
GAINS = (1.0, 0.8, 0.5, 0.4, 0.25, 0.3)
COUNTS = len(GAINS) + 1
WINDOW = 8


def sandwich_kernel(nc: bass.Bass, x: bass.AP, w_gate_t: bass.AP, w_up_t: bass.AP, w_down_t: bass.AP,
                    w_lin_t: bass.AP, lin_scale_t: bass.AP, out: bass.AP):
    TOKENS, H = x.shape
    INNER = w_gate_t.shape[1]
    TILES = TOKENS // P
    KC = H // P
    DROP = INNER // 2
    BLOCKS = -(-INNER // P)
    LAST = INNER - (BLOCKS - 1) * P
    BANKS = [(b, min(BANK, INNER - b)) for b in range(0, INNER, BANK)]
    GROUPS = [(b, min(4, BLOCKS - b)) for b in range(0, BLOCKS, 4)]
    NG = len(GROUPS)
    DOWN_LOAD = 2
    PADS = WINDOW - 1
    assert (BLOCKS - 1) % DOWN_LOAD == 0
    assert H == BANK and LAST % 32 == 0 and INNER % 2 == 0 and TILES % 2 == 0 and TILES >= 8

    x_tiles = x.rearrange("(n p) h -> n p h", p=P)
    out_tiles = out.rearrange("(n p) h -> n p h", p=P)

    with ExitStack() as ctx:
        def sb(name, shape, dt):
            return ctx.enter_context(nc.sbuf_tensor(name, shape, dt))

        def ps(name, width):
            return ctx.enter_context(nc.psum_tensor(name, [P, width], F32))

        def sem(name):
            return ctx.enter_context(nc.semaphore(name))

        low_at = -(-nc.sbuf_base // 32) * 32
        low_size = (2 * KC * INNER + BLOCKS * H + KC * H)
        weights_low = sb("weights_low", [P, low_size], F32)
        taken = [0]

        def raw_and_low(name, shape):
            words = shape[1] * shape[2]
            raw = weights_low[:, taken[0]:taken[0] + words].rearrange("p (c n) -> p c n", c=shape[1])
            low = nc.alloc_sbuf_tensor_at(name + "_lo", shape, F32R, offset=low_at + 4 * taken[0])
            taken[0] += words
            return raw, low

        gate_raw, gate_lo = raw_and_low("gate", [P, KC, INNER])
        up_raw, up_lo = raw_and_low("up", [P, KC, INNER])
        down_raw, down_lo = raw_and_low("down", [P, BLOCKS, H])
        lin_raw, lin_lo = raw_and_low("lin", [P, KC, H])
        gate_hi = sb("gate_hi", [P, KC, INNER], F32R)
        up_hi = sb("up_hi", [P, KC, INNER], F32R)
        down_hi = sb("down_hi", [P, BLOCKS, H], F32R)
        lin_hi = sb("lin_hi", [P, KC, H], F32R)
        lin_scale = sb("lin_scale", [P, KC * KC], F32)

        x_in = sb("x_in", [P, 2, H], F32)
        x_res = sb("x_res", [P, 2, H], F32)
        xT_hi = sb("xT_hi", [P, H], F32R)
        xT_lo = sb("xT_lo", [P, H], F32R)
        gated = sb("gated", [P, 2, INNER], F32)
        mag = sb("mag", [P, 2, INNER + WINDOW], F32)
        signs = sb("signs", [P, INNER + PADS], I8)
        masked = sb("masked", [P, INNER], F32)
        mT_hi = sb("mT_hi", [P, BLOCKS * P], F32R)
        mT_lo = sb("mT_lo", [P, BLOCKS * P], F32R)
        normed = sb("normed", [P, H], F32)
        x2_hat = sb("x2_hat", [P, H], F32)
        x2T_hi = sb("x2T_hi", [P, H], F32R)
        x2T_lo = sb("x2T_lo", [P, H], F32R)
        ident = sb("ident", [P, P], F32)
        ones = sb("ones", [P, 1], F32)
        busy = sb("busy", [P, 2 * P], BF16)
        unread = sb("unread", [P, 2], F32)
        eps_col = sb("eps_col", [P, 1], F32)
        neg_half = sb("neg_half", [P, 1], F32)

        thr = sb("thr", [P, 1], F32)
        thr_new = sb("thr_new", [P, 1], F32)
        moves = sb("moves", [P, 1], I32)
        mag_sum = sb("mag_sum", [P, 1], F32)
        step_unit = sb("step_unit", [P, len(GAINS)], F32)
        step = sb("step", [P, len(GAINS)], F32)
        signed = sb("signed", [P, 1], F32)
        slot_of = sb("slot_of", [P, WINDOW], F32)
        top = sb("top", [P, 1 + WINDOW], F32)
        at_thr = sb("at_thr", [P, 1], F32)
        slot = sb("slot", [P, 1], F32)
        pick = sb("pick", [P, 2, WINDOW], F32)
        drop_at = sb("drop_at", [P, 1], F32)
        above = sb("above", [P, 1], F32)
        full = sb("full", [P, 1], F32)
        bad = sb("bad", [P, 2], F32)
        bad_rows = sb("bad_rows", [1, 2], I32)
        exact = sb("exact", [P, 1], I32)
        trial = sb("trial", [P, 1], I32)
        bit = sb("bit", [P, 1], I32)
        at_least = sb("at_least", [P, 1], F32)
        carry = sb("carry", [P, 1], F32)

        class Stats:

            def __init__(self, name):
                self.parts = sb(name + "_parts", [P, 6], F32)
                self.mean_var = sb(name + "_mean_var", [P, 2], F32)
                self.var_eps = sb(name + "_var_eps", [P, 1], F32)
                self.rstd = sb(name + "_rstd", [P, 1], F32)
                self.taken = sem(name + "_stats_taken")
                self.ready = sem(name + "_rstd_ready")

        ln_in, ln_mlp, ln_mid, ln_lin = (Stats("ln_" + n) for n in ("in", "mlp", "mid", "lin"))

        ps_gate = ps("ps_gate", 3 * BANK)
        ps_up = ps("ps_up", 3 * BANK)
        ps_lin = ps("ps_lin", BANK)
        ps_down = ps("ps_down", BANK)
        FLAG = 3 * BANK - 2
        flag_sum = ps_gate[0:1, FLAG:FLAG + 2]

        gate_loaded = [sem(f"gate_loaded{c}") for c in range(KC)]
        up_loaded = [sem(f"up_loaded{c}") for c in range(KC)]
        down_loaded = [sem(f"down_loaded{n}") for n in range((BLOCKS - 1) // DOWN_LOAD + 1)]
        lin_loaded = sem("lin_loaded")
        x_in_loaded = [sem(f"x_in_loaded{b}") for b in range(2)]
        x_res_loaded = [sem(f"x_res_loaded{b}") for b in range(2)]
        out_stored = [sem(f"out_stored{b}") for b in range(2)]
        gate_hi_ready, gate_lo_ready = sem("gate_hi_ready"), sem("gate_lo_ready")
        up_hi_ready, up_lo_ready = sem("up_hi_ready"), sem("up_lo_ready")
        down_hi_ready, down_lo_ready = sem("down_hi_ready"), sem("down_lo_ready")
        lin_scaled, lin_hi_ready, lin_lo_ready = sem("lin_scaled"), sem("lin_hi_ready"), sem("lin_lo_ready")
        pool_set, ident_ready, consts_ready = sem("pool_set"), sem("ident_ready"), sem("consts_ready")
        x_hat_ready = sem("x_hat_ready")
        xT_done, xT_hi_ready, xT_lo_ready = sem("xT_done"), sem("xT_hi_ready"), sem("xT_lo_ready")
        gate_done, up_done = sem("gate_done"), sem("up_done")
        silu_ready, mag_ready = sem("silu_ready"), sem("mag_ready")
        thr_ready, counted = sem("thr_ready"), sem("counted")
        bad_ready, flag_done = sem("bad_ready"), sem("flag_done")
        product_ready, masked_ready = sem("product_ready"), sem("masked_ready")
        mT_done, mT_hi_ready, mT_lo_ready = sem("mT_done"), sem("mT_hi_ready"), sem("mT_lo_ready")
        down_done, down_read = sem("down_done"), sem("down_read")
        x2_hat_ready = sem("x2_hat_ready")
        x2T_done, x2T_hi_ready, x2T_lo_ready = sem("x2T_done"), sem("x2T_hi_ready"), sem("x2T_lo_ready")
        lin_done, lin_read, out_ready = sem("lin_done"), sem("lin_read"), sem("out_ready")

        def each_iteration(eng, iteration):
            def known(i):
                iteration(i, i % 2, lambda d: 0 <= i + d < TILES)
            for i in range(4):
                known(i)
            with eng.Fori(2, TILES // 2 - 1) as pair:
                for b in range(2):
                    iteration(pair * 2 + b, b, lambda d: True)
            for i in range(TILES - 2, TILES + 2):
                known(i)

        EARLY_DOWN = COUNTS - 1

        def is_number(i):
            return isinstance(i, int)

        def is_first(i):
            return is_number(i) and i == 0

        def is_second(i):
            return is_number(i) and i == 1

        def ramp(i):
            return is_first(i) or is_second(i)

        def precedes_end(i):
            return is_number(i) and i == TILES - 2

        def ends(i):
            return is_number(i) and i == TILES - 1

        def is_tail(i):
            return is_number(i) and i == TILES

        def is_last(i):
            return is_number(i) and i == TILES + 1

        def down_bank(n):
            return ps_up[:, BANK:BANK + H] if is_number(n) and n == TILES - 1 else ps_down[:, :]

        def x2T_bank(n):
            return ps_up[:, 0:H] if is_number(n) and n == TILES - 1 else ps_lin[:, :]

        def wait(eng, semaphore, value):
            if not isinstance(value, int) or value > 0:
                eng.wait_ge(semaphore, value)

        block = ctx.enter_context(nc.Block())

        @block.sync
        def _(sp):
            def load_x_in(n, b):
                sp.dma_start(x_in[:, b, :], x_tiles[n]).then_inc(x_in_loaded[b], 16)

            def load_x_res(n, b):
                sp.dma_start(x_res[:, b, :], x_tiles[n]).then_inc(x_res_loaded[b], 16)

            load_x_in(0, 0)
            for c in range(KC):
                sp.dma_start(gate_raw[:, c, :], w_gate_t[c * P:(c + 1) * P, :]).then_inc(gate_loaded[c], 16)
            load_x_in(1, 1)
            for c in range(KC):
                sp.dma_start(up_raw[:, c, :], w_up_t[c * P:(c + 1) * P, :]).then_inc(up_loaded[c], 16)
            full = (BLOCKS - 1) * P
            for n, c0 in enumerate(range(0, BLOCKS - 1, DOWN_LOAD)):
                c1 = min(c0 + DOWN_LOAD, BLOCKS - 1)
                sp.dma_start(down_raw[:, c0:c1, :],
                             w_down_t[c0 * P:c1 * P, :].rearrange("(c p) h -> p c h", p=P)
                             ).then_inc(down_loaded[n], 16)
            sp.dma_start(down_raw[0:LAST, BLOCKS - 1, :], w_down_t[full:INNER, :]).then_inc(down_loaded[-1], 16)
            sp.wait_ge(xT_done, 1)
            load_x_in(2, 0)
            load_x_res(0, 0)
            load_x_res(1, 1)
            sp.dma_start(lin_scale[:, :], lin_scale_t.rearrange("(o n) -> o n", o=1).to_broadcast([P, KC * KC])
                         ).then_inc(lin_loaded, 16)
            sp.dma_start(lin_raw[:, :, :], w_lin_t.rearrange("(c p) h -> p c h", p=P)).then_inc(lin_loaded, 16)

            def iteration(i, b, has):
                if has(2) and not is_first(i):
                    sp.wait_ge(xT_done, i + 1)
                    load_x_in(i + 2, b)
                if has(-2):
                    sp.wait_ge(out_ready, i - 1)
                    sp.dma_start(out_tiles[i - 2], x_res[:, b, :]).then_inc(out_stored[b], 16)
                    if has(0):
                        sp.wait_ge(out_stored[b], (i - b) * 8)
                        load_x_res(i, b)

            each_iteration(sp, iteration)
            for b in range(2):
                sp.wait_ge(out_stored[b], 16 * (TILES // 2))

        @block.gpsimd
        def _(pool):
            nc.gpsimd.memset(ident[:, :], 0.0).then_inc(pool_set, 1)
            nc.gpsimd.memset(eps_col[:, :], EPS).then_inc(pool_set, 1)
            nc.gpsimd.memset(neg_half[:, :], -0.5).then_inc(pool_set, 1)
            pool.wait_ge(pool_set, 3)
            nc.gpsimd.affine_select(out=ident[:, :], in_=ident[:, :], compare_op=ALU.not_equal, fill=1.0, base=0,
                                    pattern=[[-1, P]], channel_multiplier=1).then_inc(ident_ready, 1)

            def rstd(ln, n):
                pool.wait_ge(ln.taken, n + 1)
                nc.gpsimd.tensor_tensor(ln.var_eps[:, :], ln.mean_var[:, 1:2], eps_col[:, :], ALU.add)
                pool.drain()
                nc.gpsimd.tensor_tensor(ln.rstd[:, :], ln.var_eps[:, :], neg_half[:, :], ALU.pow).then_inc(ln.ready, 1)

            def low_part(lo, raw, hi):
                return nc.gpsimd.tensor_tensor(lo, raw, hi.bitcast(F32), ALU.subtract)

            def second_residual(n, b):
                pool.wait_ge(lin_read, n + 1)
                nc.gpsimd.tensor_tensor(x_res[:, b, :], x_res[:, b, :], normed[:, :], ALU.add).then_inc(out_ready, 1)

            def iteration(i, b, has):
                if is_first(i):
                    down_low(range(EARLY_DOWN - 1))
                if is_second(i):
                    down_low(range(EARLY_DOWN, BLOCKS))
                    scale_lin()
                if is_tail(i):
                    rstd(ln_lin, i - 3)
                    second_residual(i - 3, 1 - b)
                if has(-2):
                    rstd(ln_mlp, i - 2)
                    rstd(ln_mid, i - 2)
                if is_number(i) and i == 2:
                    lin_low()
                if has(1) and has(-2):
                    rstd(ln_lin, i - 2)
                if has(2):
                    rstd(ln_in, i + 2)
                if is_first(i):
                    down_low(range(EARLY_DOWN - 1, EARLY_DOWN))
                if has(1) and has(-2):
                    second_residual(i - 2, b)
                if is_last(i):
                    rstd(ln_lin, i - 3)
                    second_residual(i - 3, 1 - b)
                    rstd(ln_lin, i - 2)

            rstd(ln_in, 0)
            rstd(ln_in, 1)

            def down_low(blocks):
                for c in blocks:
                    rows = min(P, INNER - c * P)
                    pool.wait_ge(down_hi_ready, c + 1)
                    low_part(down_lo[0:rows, c, :], down_raw[0:rows, c, :],
                             down_hi[0:rows, c, :]).then_inc(down_lo_ready, 1)

            def scale_lin():
                pool.wait_ge(lin_loaded, 32)
                lin_blocks = lin_raw.rearrange("p c (o n) -> p (c o) n", n=P)
                nc.gpsimd.tensor_tensor(lin_blocks, lin_blocks,
                                        lin_scale[:, :].unsqueeze(2).to_broadcast([P, KC * KC, P]),
                                        ALU.mult).then_inc(lin_scaled, 1)

            def lin_low():
                pool.wait_ge(lin_hi_ready, KC)
                low_part(lin_lo[:, :, :], lin_raw, lin_hi[:, :, :]).then_inc(lin_lo_ready, 1)

            each_iteration(pool, iteration)

        @block.scalar
        def _(act):
            def high_part(hi, src):
                return nc.scalar.activation(hi, src, ACT.Copy)

            def gate_high(c):
                act.wait_ge(gate_loaded[c], 16)
                high_part(gate_hi[:, c, :], gate_raw[:, c, :]).then_inc(gate_hi_ready, 1)

            def xT_high(n):
                act.wait_ge(xT_done, n + 1)
                high_part(xT_hi[:, :], ps_down[:, :]).then_inc(xT_hi_ready, 1)

            act.wait_ge(consts_ready, 1)
            nc.scalar.activation(unread[:, 1:2], ones[:, :], ACT.Silu)
            gate_high(0)
            xT_high(0)
            for c in range(1, KC):
                gate_high(c)

            def up_high(c):
                act.wait_ge(up_loaded[c], 16)
                high_part(up_hi[:, c, :], up_raw[:, c, :]).then_inc(up_hi_ready, 1)

            def down_high(c):
                rows = min(P, INNER - c * P)
                act.wait_ge(down_loaded[c // DOWN_LOAD], 16)
                high_part(down_hi[0:rows, c, :], down_raw[0:rows, c, :]).then_inc(down_hi_ready, 1)

            for c in range(KC - 1):
                up_high(c)

            def iteration(i, b, has):
                def count(k):
                    act.wait_ge(thr_ready, i * COUNTS + k + 1)
                    nc.scalar.activation(signs[:, :], mag[:, b, 0:INNER + PADS], ACT.Sign, bias=thr[:, :],
                                         scale=-1.0, accum_out=signed[:, :]).then_inc(counted, 1)

                def mT_high(g):
                    c0, cn = GROUPS[g]
                    act.wait_ge(mT_done, (i - 1) * NG + g + 1)
                    if g == 0:
                        wait(act, down_done, i - 1)
                    high_part(mT_hi[:, c0 * P:(c0 + cn) * P], ps_gate[:, c0 * P:(c0 + cn) * P]
                              ).then_inc(mT_hi_ready, 1)

                def x2T_high():
                    act.wait_ge(x2T_done, i - 1)
                    if is_last(i):
                        act.wait_ge(lin_done, i - 2)
                    high_part(x2T_hi[:, :], x2T_bank(i - 2)).then_inc(x2T_hi_ready, 1)

                if has(0):
                    act.wait_ge(gate_done, i + 1)
                    wait(act, masked_ready, i - 1)
                    nc.scalar.activation(gated[:, b, :], ps_gate[:, 0:INNER], ACT.Silu).then_inc(silu_ready, 1)
                    if is_first(i):
                        up_high(KC - 1)
                    act.wait_ge(silu_ready, i + 1)
                    nc.scalar.activation(mag[:, b, 0:INNER], gated[:, b, :], ACT.Abs,
                                         accum_out=mag_sum[:, :]).then_inc(mag_ready, 1)
                    if is_second(i):
                        for c in range(EARLY_DOWN, BLOCKS):
                            down_high(c)
                    count(0)
                if ends(i):
                    for k in range(1, 4):
                        count(k)
                    x2T_high()
                    count(4)
                    mT_high(0)
                    count(5)
                    mT_high(1)
                    mT_high(2)
                    count(6)
                    return
                if ramp(i):
                    xT_high(i + 1)
                if is_second(i):
                    mT_high(0)
                if has(-2) and not is_tail(i):
                    x2T_high()
                if has(0):
                    count(1)
                if is_first(i):
                    down_high(0)
                if has(1) and not ramp(i):
                    xT_high(i + 1)
                if has(-1) and not is_second(i):
                    mT_high(0)
                for k in range(2, COUNTS):
                    if has(0):
                        count(k)
                    if has(-1) and k - 1 < NG and not (precedes_end(i) and k == NG):
                        mT_high(k - 1)
                        if precedes_end(i) and k == NG - 1:
                            mT_high(NG - 1)
                    if is_first(i):
                        down_high(k - 1)
                    if is_second(i) and k >= COUNTS - KC:
                        c = k - (COUNTS - KC)
                        act.wait_ge(lin_scaled, 1)
                        high_part(lin_hi[:, c, :], lin_raw[:, c, :]).then_inc(lin_hi_ready, 1)
                if is_tail(i):
                    x2T_high()

            assert NG == 3 and COUNTS == 7 and KC <= COUNTS - 2 and EARLY_DOWN <= BLOCKS
            each_iteration(act, iteration)

        @block.vector
        def _(dve):
            V = nc.vector
            for b in range(2):
                V.memset(mag[:, b, INNER:INNER + WINDOW], 3e38)
            V.memset(ones[:, :], 1.0)
            V.memset(busy[:, :], 1.0)
            for k, gain in enumerate(GAINS):
                V.memset(step_unit[:, k:k + 1], -gain * SPACING_PER_MEAN / INNER / 2)
            for r in range(WINDOW):
                V.memset(slot_of[:, r:r + 1], float(2 * r - PADS))
            V.memset(top[:, 0:1], 3e38)
            V.memset(ps_gate[:, INNER:3 * BANK], 0.0).then_inc(consts_ready, 1)

            def take_stats(ln, src):
                V.bn_stats(ln.parts[:, :], src)
                dve.drain()
                V.bn_aggr(ln.mean_var[:, :], ln.parts[:, :]).then_inc(ln.taken, 1)

            def normalise(dst, src, ln, n):
                dve.wait_ge(ln.ready, n + 1)
                return V.tensor_scalar(dst, src, ln.mean_var[:, 0:1], ln.rstd[:, :], ALU.subtract, ALU.mult)

            def low_part(lo, src, hi):
                return V.tensor_tensor(lo, src, hi.bitcast(F32), ALU.subtract)

            def stats_in(n, b):
                dve.wait_ge(x_in_loaded[b], (n - b) * 8 + 16)
                take_stats(ln_in, x_in[:, b, :])

            def x_hat(n, b):
                normalise(x_in[:, b, :], x_in[:, b, :], ln_in, n).then_inc(x_hat_ready, 1)

            def xT_low(n):
                dve.wait_ge(xT_hi_ready, n + 1)
                low_part(xT_lo[:, :], ps_down[:, :], xT_hi[:, :]).then_inc(xT_lo_ready, 1)

            def exact_search(b, numbers):
                a = mag[:, b, 0:INNER]
                scratch = masked[:, :].bitcast(BF16)[:, 0:INNER]
                value = exact[:, :].bitcast(F32)
                V.tensor_copy(value, drop_at[:, :])
                dve.drain()
                unsearched = dve.value_load(bad_rows[0:1, 1:2], min_val=0, max_val=2 * P)
                with dve.If(unsearched > 0):
                    V.memset(exact[:, :], 0)
                    V.memset(bit[:, :], 1 << 30)
                    dve.drain()
                    with dve.Fori(0, 31):
                        V.tensor_tensor(trial[:, :], exact[:, :], bit[:, :], ALU.bitwise_or)
                        dve.drain()
                        V.tensor_scalar(scratch, a, trial[:, :].bitcast(F32), None, ALU.is_ge, ALU.add,
                                        accum_out=at_least[:, :])
                        V.tensor_scalar(bit[:, :], bit[:, :], 1, None, ALU.logical_shift_right)
                        dve.drain()
                        V.tensor_scalar(moves[:, :], at_least[:, :], float(INNER - DROP + 1), None, ALU.is_ge)
                        dve.drain()
                        V.copy_predicated(exact[:, :], moves[:, :], trial[:, :])
                        dve.drain()
                dve.drain()
                V.tensor_scalar(scratch, a, value, None, ALU.is_ge, ALU.add, accum_out=at_least[:, :])
                V.memset(carry[:, :], 0.0)
                dve.drain()
                V.tensor_scalar(at_least[:, :], at_least[:, :], float(INNER - DROP), None, ALU.subtract)
                V.tensor_scalar(masked[:, :], a, value, None, ALU.is_equal)
                dve.drain()
                for c0, cn in BANKS:
                    equal, kept, number = masked[:, c0:c0 + cn], mag[:, b, c0:c0 + cn], numbers[:, 0:cn]
                    V.tensor_tensor_scan(number, equal, equal, carry[:, :], ALU.add, ALU.max)
                    dve.drain()
                    V.tensor_copy(carry[:, :], numbers[:, cn - 1:cn])
                    V.tensor_tensor(equal, number, equal, ALU.mult)
                    dve.drain()
                    V.tensor_scalar(equal, equal, at_least[:, :], None, ALU.is_gt)
                    dve.drain()
                    V.scalar_tensor_tensor(kept, kept, value, equal, ALU.is_gt, ALU.add)
                    dve.drain()
                V.memset(drop_at[:, :], 0.5)
                dve.drain()

            def up_low(c):
                dve.wait_ge(up_hi_ready, c + 1)
                low_part(up_lo[:, c, :], up_raw[:, c, :], up_hi[:, c, :]).then_inc(up_lo_ready, 1)

            stats_in(0, 0)
            x_hat(0, 0)
            for c in range(KC):
                dve.wait_ge(gate_hi_ready, c + 1)
                low_part(gate_lo[:, c, :], gate_raw[:, c, :], gate_hi[:, c, :]).then_inc(gate_lo_ready, 1)
                if c == 0:
                    xT_low(0)
            for c in range(KC - 1):
                up_low(c)
            stats_in(1, 1)
            up_low(KC - 1)
            x_hat(1, 1)

            def iteration(i, b, has):
                first = is_first(i)

                def start_threshold():
                    dve.wait_ge(mag_ready, i + 1)
                    V.tensor_scalar(step[:, :], step_unit[:, :], mag_sum[:, :], None, ALU.mult)
                    V.tensor_scalar(thr[:, :], mag_sum[:, :], MEDIAN_PER_MEAN / INNER, None,
                                    ALU.mult).then_inc(thr_ready, 1)

                def move_threshold(k):
                    dve.wait_ge(counted, i * COUNTS + k + 1)
                    V.tensor_scalar(moves[:, :], signed[:, :], signed[:, :], (PADS + 0.5) ** 2, ALU.mult, ALU.is_gt)
                    V.scalar_tensor_tensor(thr_new[:, :], signed[:, :], step[:, k:k + 1], thr[:, :],
                                           ALU.mult, ALU.add)
                    dve.drain()
                    V.copy_predicated(thr[:, :], moves[:, :], thr_new[:, :]).then_inc(thr_ready, 1)

                def mT_low(g):
                    c0, cn = GROUPS[g]
                    cols = slice(c0 * P, (c0 + cn) * P)
                    dve.wait_ge(mT_hi_ready, (i - 1) * NG + g + 1)
                    low_part(mT_lo[:, cols], ps_gate[:, cols], mT_hi[:, cols]).then_inc(mT_lo_ready, 1)

                def first_residual():
                    wait(dve, out_ready, i - 3 if is_last(i) else i - 2)
                    normalise(normed[:, :], down_bank(i - 2), ln_mlp, i - 2).then_inc(down_read, 1)
                    dve.drain()
                    dve.wait_ge(x_res_loaded[b], (i - b) * 8)
                    V.tensor_tensor(x_res[:, b, :], x_res[:, b, :], normed[:, :], ALU.add)

                def second_norm():
                    wait(dve, x2T_done, i - 2)
                    normalise(x2_hat[:, :], x_res[:, b, :], ln_mid, i - 2).then_inc(x2_hat_ready, 1)

                def x2T_low(n):
                    dve.wait_ge(x2T_hi_ready, n + 1)
                    low_part(x2T_lo[:, :], x2T_bank(n), x2T_hi[:, :]).then_inc(x2T_lo_ready, 1)

                def keep():
                    V.scalar_tensor_tensor(masked[:, :], mag[:, 1 - b, 0:INNER], drop_at[:, :], gated[:, 1 - b, :],
                                           ALU.is_gt, ALU.mult)

                def largest_below():
                    dve.drain()
                    wait(dve, mT_done, i * NG)
                    V.scalar_tensor_tensor(masked[:, :], mag[:, b, 0:INNER], thr[:, :], mag[:, b, 0:INNER],
                                           ALU.is_le, ALU.mult)
                    if ends(i):
                        mT_low(1)
                    dve.drain()
                    V.max(top[:, 1:], masked[:, :])
                    if ends(i):
                        mT_low(2)
                    dve.drain()
                    V.tensor_scalar(pick[:, 0, :], top[:, 1:], thr[:, :], None, ALU.is_equal, ALU.add,
                                    accum_out=at_thr[:, :])
                    V.tensor_tensor(full[:, :], top[:, WINDOW:], thr[:, :], ALU.is_ge)
                    dve.drain()

                def linear_stats(n):
                    dve.wait_ge(lin_done, n + 1)
                    take_stats(ln_lin, ps_lin[:, :])

                def down_stats():
                    dve.wait_ge(down_done, i - 1)
                    take_stats(ln_mlp, down_bank(i - 2))

                def settle():
                    dve.wait_ge(counted, i * COUNTS)
                    V.tensor_tensor(slot[:, :], signed[:, :], at_thr[:, :], ALU.add)
                    dve.drain()
                    V.scalar_tensor_tensor(pick[:, 0, :], slot_of[:, :], slot[:, :], top[:, 1:], ALU.is_equal,
                                           ALU.mult, accum_out=drop_at[:, :])
                    V.scalar_tensor_tensor(pick[:, 1, :], slot_of[:, :], slot[:, :], top[:, 0:WINDOW], ALU.is_equal,
                                           ALU.mult, accum_out=above[:, :])
                    dve.drain()
                    V.scalar_tensor_tensor(bad[:, 0:1], drop_at[:, :], above[:, :], full[:, :], ALU.is_ge, ALU.add)
                    V.scalar_tensor_tensor(bad[:, 1:2], above[:, :], 0.0, full[:, :], ALU.is_equal,
                                           ALU.add).then_inc(bad_ready, 1)

                def hand_over_masked():
                    dve.wait_ge(flag_done, i)
                    V.tensor_copy(bad_rows[:, :], flag_sum)
                    dve.drain()
                    unsettled = dve.value_load(bad_rows[0:1, 0:1], min_val=0, max_val=2 * P)
                    with dve.If(unsettled > 0):
                        exact_search(1 - b, x_in[:, 0, :] if is_tail(i) else normed[:, :])
                        keep()
                        dve.drain()
                    V.tensor_copy(unread[:, 0:1], ones[:, :]).then_inc(masked_ready, 1)

                def middle_stats():
                    dve.drain()
                    take_stats(ln_mid, x_res[:, b, :])

                def make_product():
                    dve.wait_ge(up_done, i + 1)
                    V.tensor_tensor(gated[:, b, :], gated[:, b, :], ps_up[:, 0:INNER],
                                    ALU.mult).then_inc(product_ready, 1)

                def linear_norm(n):
                    normalise(normed[:, :], ps_lin[:, :], ln_lin, n).then_inc(lin_read, 1)

                if ends(i):
                    settle()
                    keep()
                    start_threshold()
                    down_stats()
                    move_threshold(0)
                    first_residual()
                    move_threshold(1)
                    middle_stats()
                    move_threshold(2)
                    hand_over_masked()
                    second_norm()
                    move_threshold(3)
                    x2T_low(i - 2)
                    make_product()
                    move_threshold(4)
                    mT_low(0)
                    move_threshold(5)
                    largest_below()
                elif is_tail(i):
                    settle()
                    keep()
                    hand_over_masked()
                    linear_stats(i - 3)
                    mT_low(0)
                    linear_norm(i - 3)
                    mT_low(1)
                    mT_low(2)
                    down_stats()
                    first_residual()
                    middle_stats()
                    second_norm()
                elif is_last(i):
                    down_stats()
                    x2T_low(i - 3)
                    first_residual()
                    middle_stats()
                    linear_stats(i - 3)
                    second_norm()
                    linear_norm(i - 3)
                    x2T_low(i - 2)
                    linear_stats(i - 2)
                    dve.wait_ge(out_ready, i - 2)
                    normalise(normed[:, :], ps_lin[:, :], ln_lin, i - 2)
                    dve.drain()
                    V.tensor_tensor(x_res[:, b, :], x_res[:, b, :], normed[:, :], ALU.add).then_inc(out_ready, 1)
                else:
                    if has(-2):
                        down_stats()
                    if has(-1):
                        settle()
                    if has(-2):
                        first_residual()
                        middle_stats()
                    if has(-1):
                        keep()
                    if has(-2):
                        second_norm()
                    start_threshold()
                    if has(-1):
                        hand_over_masked()
                    move_threshold(0)
                    if ramp(i):
                        xT_low(i + 1)
                    if is_second(i):
                        mT_low(0)
                    if has(-2):
                        x2T_low(i - 2)
                    move_threshold(1)
                    if not ramp(i):
                        xT_low(i + 1)
                    if has(-1) and not is_second(i):
                        mT_low(0)
                    move_threshold(2)
                    if has(-1):
                        mT_low(1)
                    if precedes_end(i):
                        mT_low(2)
                    make_product()
                    move_threshold(3)
                    if has(-1) and not precedes_end(i):
                        mT_low(2)
                    if has(-2):
                        linear_stats(i - 2)
                    move_threshold(4)
                    if has(2):
                        stats_in(i + 2, b)
                    if has(-2):
                        linear_norm(i - 2)
                    move_threshold(5)
                    largest_below()
                    if has(2):
                        x_hat(i + 2, b)

            each_iteration(dve, iteration)

        @block.tensor
        def _(pe):
            def product(parts, lhs_hi, lhs_lo, first, last):
                for dst, rhs_hi, rhs_lo in parts:
                    nc.tensor.matmul(dst, lhs_hi, rhs_hi, start=first, stop=False)
                    nc.tensor.matmul(dst, lhs_hi, rhs_lo, start=False, stop=False)
                for dst, rhs_hi, _ in parts:
                    mm = nc.tensor.matmul(dst, lhs_lo, rhs_hi, start=False, stop=last)
                return mm

            def transpose_rows(dst, src):
                for c in range(KC):
                    last = nc.tensor.transpose(dst[:, c * P:(c + 1) * P], src[:, c * P:(c + 1) * P], ident[:, :])
                return last

            def xT(n, b):
                pe.wait_ge(x_hat_ready, n + 1)
                transpose_rows(ps_down, x_in[:, b, :]).then_inc(xT_done, 1)

            def wide(dst, w_hi, w_lo, c):
                k = slice(c * P, (c + 1) * P)
                cols = [slice(c0, c0 + cn) for c0, cn in BANKS]
                return product([(dst[:, s], w_hi[:, c, s], w_lo[:, c, s]) for s in cols],
                               xT_hi[:, k], xT_lo[:, k], c == 0, c == KC - 1)

            def keep_clock(matmuls):
                for _ in range(matmuls):
                    nc.tensor.matmul(ps_up[:, 2 * BANK:2 * BANK + 2 * P], busy[:, 0:P], busy[:, :], start=True, stop=True)

            pe.wait_ge(consts_ready, 1)
            keep_clock(15)
            pe.wait_ge(ident_ready, 1)
            xT(0, 0)
            keep_clock(22)

            def iteration(i, b, has):
                first = is_first(i)

                def gate(n):
                    pe.wait_ge(xT_hi_ready, n + 1)
                    pe.wait_ge(xT_lo_ready, n + 1)
                    wait(pe, mT_lo_ready, (n - 1) * NG)
                    for c in range(KC):
                        if first:
                            pe.wait_ge(gate_hi_ready, c + 1)
                            pe.wait_ge(gate_lo_ready, c + 1)
                        last = wide(ps_gate, gate_hi, gate_lo, c)
                    last.then_inc(gate_done, 1)

                if has(0):
                    if not ends(i):
                        gate(i)
                    wait(pe, product_ready, i)

                def up(c):
                    if first:
                        pe.wait_ge(up_hi_ready, c + 1)
                        pe.wait_ge(up_lo_ready, c + 1)
                    return wide(ps_up, up_hi, up_lo, c)

                def flag(n):
                    pe.wait_ge(bad_ready, n + 1)
                    if not is_number(n) or n < TILES - 1:
                        pe.wait_ge(silu_ready, n + 2)
                    nc.tensor.matmul(flag_sum, ones[:, :], bad[:, :], start=True, stop=True).then_inc(flag_done, 1)

                def linear():
                    pe.wait_ge(x2T_hi_ready, i - 1)
                    pe.wait_ge(x2T_lo_ready, i - 1)
                    if is_number(i) and i == 2:
                        pe.wait_ge(lin_hi_ready, KC)
                        pe.wait_ge(lin_lo_ready, 1)
                    for c in range(KC):
                        k = slice(c * P, (c + 1) * P)
                        last = product([(ps_lin[:, :], lin_hi[:, c, :], lin_lo[:, c, :])], x2T_hi[:, k], x2T_lo[:, k],
                                       c == 0, c == KC - 1)
                    last.then_inc(lin_done, 1)

                def transpose_second_norm():
                    pe.wait_ge(x2_hat_ready, i - 1)
                    if not is_last(i):
                        wait(pe, lin_read, i - 2)
                    transpose_rows(x2T_bank(i - 2), x2_hat).then_inc(x2T_done, 1)

                if has(0):
                    up(0)
                if has(-1) and has(0) and not is_second(i) and not ends(i):
                    flag(i - 1)
                if is_tail(i):
                    pe.wait_ge(product_ready, TILES)
                if has(0):
                    up(1)
                if has(-2) and not is_tail(i) and not ends(i):
                    transpose_second_norm()
                if is_last(i):
                    keep_clock(15)
                    pe.wait_ge(lin_read, i - 2)
                    linear()
                if has(0):
                    if ends(i):
                        flag(i - 1)
                    up(2)
                    up(3).then_inc(up_done, 1)
                if is_second(i):
                    flag(i - 1)
                if has(1):
                    if first:
                        pe.wait_ge(xT_lo_ready, 1)
                    wait(pe, down_read, i - 1)
                    xT(i + 1, 1 - b)
                if ends(i):
                    transpose_second_norm()
                if has(-1):
                    pe.wait_ge(masked_ready, i)
                    for c0, cn in GROUPS:
                        for c in range(c0, c0 + cn):
                            rows = min(P, INNER - c * P)
                            last = nc.tensor.transpose(ps_gate[0:rows, c * P:(c + 1) * P],
                                                       masked[:, c * P:c * P + rows], ident[:, :])
                        last.then_inc(mT_done, 1)
                if has(-2) and has(0):
                    linear()
                if has(-1):
                    if has(1):
                        pe.wait_ge(xT_lo_ready, i + 2)
                    elif not is_tail(i):
                        pe.wait_ge(down_read, i - 1)
                    for g, (c0, cn) in enumerate(GROUPS):
                        pe.wait_ge(mT_hi_ready, (i - 1) * NG + g + 1)
                        pe.wait_ge(mT_lo_ready, (i - 1) * NG + g + 1)
                        for c in range(c0, c0 + cn):
                            rows = min(P, INNER - c * P)
                            k = slice(c * P, (c + 1) * P)
                            if is_second(i):
                                pe.wait_ge(down_hi_ready, c + 1)
                                pe.wait_ge(down_lo_ready, c + 1)
                            last = product([(down_bank(i - 1), down_hi[0:rows, c, :], down_lo[0:rows, c, :])],
                                           mT_hi[0:rows, k], mT_lo[0:rows, k], c == 0, c == BLOCKS - 1)
                        if precedes_end(i) and g == 0:
                            gate(i + 1)
                        if ends(i) and g == NG - 2:
                            flag(i)
                    last.then_inc(down_done, 1)
                if is_tail(i):
                    transpose_second_norm()
                    linear()
                    keep_clock(12)

            each_iteration(pe, iteration)


def kernel(L0_attn_x, L0_attn_w_gate, L0_attn_w_up, L0_attn_w_down, L0_ffn_weight, L0_ffn_weight_scale):
    import numpy as np
    import concourse.bacc as bacc
    from concourse.bass_utils import run_bass_kernel_spmd

    nc = bacc.Bacc("TRN2", target_bir_lowering=False, num_devices=1)
    x = np.asarray(L0_attn_x)
    arrays = {
        "x": x.reshape(-1, x.shape[-1]),
        "w_gate_t": np.ascontiguousarray(np.asarray(L0_attn_w_gate).T),
        "w_up_t": np.ascontiguousarray(np.asarray(L0_attn_w_up).T),
        "w_down_t": np.ascontiguousarray(np.asarray(L0_attn_w_down).T),
        "w_lin_t": np.ascontiguousarray(np.asarray(L0_ffn_weight).T),
        "lin_scale_t": np.ascontiguousarray(np.asarray(L0_ffn_weight_scale).T).reshape(-1),
    }
    aps = [nc.dram_tensor(n + "_dram", a.shape, mybir.dt.from_np(a.dtype), kind="ExternalInput").ap()
           for n, a in arrays.items()]
    out = nc.dram_tensor("out_dram", arrays["x"].shape, F32, kind="ExternalOutput").ap()
    sandwich_kernel(nc, *aps, out)
    r = run_bass_kernel_spmd(nc, [{n + "_dram": a for n, a in arrays.items()}], core_ids=[0])
    return r.results[0]["out_dram"].reshape(x.shape)
```
